# Optimizing a Trainium2 kernel written in Bass

```python
import numpy as np
import jax
import jax.numpy as jnp

def _softmax(x, axis=-1):
    return jax.nn.softmax(x, axis=axis)

def _gelu(x):
    return jax.nn.gelu(x, approximate=True)

def _silu(x):
    return jax.nn.silu(x)

def _sigmoid(x):
    return jax.nn.sigmoid(x)

def _layernorm(x, axis=-1, eps=1e-05):
    m = jnp.mean(x, axis=axis, keepdims=True)
    v = jnp.var(x, axis=axis, keepdims=True)
    return (x - m) / jnp.sqrt(v + eps)

def _scatter_add(tgt, idx, src, axis=0):
    return tgt.at[idx].add(src)

def _segment_sum(src, seg, n):
    return jax.ops.segment_sum(src, seg, n)
kernel_name = 'mk_dlrm_tower_d1_rec_r8_2dd2ba'

def setup_inputs(seed: int=0):
    np.random.seed(seed)
    _w = jnp.asarray

    def _rec_inputs():
        import jax
        import jax.numpy as jnp
        _tk = jax.random.key(seed)
        dense_ctx = jax.random.normal(jax.random.fold_in(_tk, 190), (512, 16), jnp.float32)
        ids = jnp.stack([jax.random.randint(jax.random.fold_in(_tk, 200 + f), (512,), 0, v, jnp.int32) for f, v in enumerate([1000, 1250, 125000, 1000, 1000, 1000, 1000, 125000, 1000, 12500, 12500, 12500, 1000, 1000, 1250, 125000, 1250, 1250, 1000, 12500, 125000, 12500, 1250, 125000, 125000, 125000, 1000, 1000, 1250, 1000, 1000, 1250])], axis=1)
        tbl_0 = 0.05 * jax.random.normal(jax.random.fold_in(_tk, 500 + 0), (1000, 16), jnp.float32)
        tbl_1 = 0.05 * jax.random.normal(jax.random.fold_in(_tk, 500 + 1), (1250, 16), jnp.float32)
        tbl_2 = 0.05 * jax.random.normal(jax.random.fold_in(_tk, 500 + 2), (125000, 16), jnp.float32)
        tbl_3 = 0.05 * jax.random.normal(jax.random.fold_in(_tk, 500 + 3), (1000, 16), jnp.float32)
        tbl_4 = 0.05 * jax.random.normal(jax.random.fold_in(_tk, 500 + 4), (1000, 16), jnp.float32)
        tbl_5 = 0.05 * jax.random.normal(jax.random.fold_in(_tk, 500 + 5), (1000, 16), jnp.float32)
        tbl_6 = 0.05 * jax.random.normal(jax.random.fold_in(_tk, 500 + 6), (1000, 16), jnp.float32)
        tbl_7 = 0.05 * jax.random.normal(jax.random.fold_in(_tk, 500 + 7), (125000, 16), jnp.float32)
        tbl_8 = 0.05 * jax.random.normal(jax.random.fold_in(_tk, 500 + 8), (1000, 16), jnp.float32)
        tbl_9 = 0.05 * jax.random.normal(jax.random.fold_in(_tk, 500 + 9), (12500, 16), jnp.float32)
        tbl_10 = 0.05 * jax.random.normal(jax.random.fold_in(_tk, 500 + 10), (12500, 16), jnp.float32)
        tbl_11 = 0.05 * jax.random.normal(jax.random.fold_in(_tk, 500 + 11), (12500, 16), jnp.float32)
        tbl_12 = 0.05 * jax.random.normal(jax.random.fold_in(_tk, 500 + 12), (1000, 16), jnp.float32)
        tbl_13 = 0.05 * jax.random.normal(jax.random.fold_in(_tk, 500 + 13), (1000, 16), jnp.float32)
        tbl_14 = 0.05 * jax.random.normal(jax.random.fold_in(_tk, 500 + 14), (1250, 16), jnp.float32)
        tbl_15 = 0.05 * jax.random.normal(jax.random.fold_in(_tk, 500 + 15), (125000, 16), jnp.float32)
        tbl_16 = 0.05 * jax.random.normal(jax.random.fold_in(_tk, 500 + 16), (1250, 16), jnp.float32)
        tbl_17 = 0.05 * jax.random.normal(jax.random.fold_in(_tk, 500 + 17), (1250, 16), jnp.float32)
        tbl_18 = 0.05 * jax.random.normal(jax.random.fold_in(_tk, 500 + 18), (1000, 16), jnp.float32)
        tbl_19 = 0.05 * jax.random.normal(jax.random.fold_in(_tk, 500 + 19), (12500, 16), jnp.float32)
        tbl_20 = 0.05 * jax.random.normal(jax.random.fold_in(_tk, 500 + 20), (125000, 16), jnp.float32)
        tbl_21 = 0.05 * jax.random.normal(jax.random.fold_in(_tk, 500 + 21), (12500, 16), jnp.float32)
        tbl_22 = 0.05 * jax.random.normal(jax.random.fold_in(_tk, 500 + 22), (1250, 16), jnp.float32)
        tbl_23 = 0.05 * jax.random.normal(jax.random.fold_in(_tk, 500 + 23), (125000, 16), jnp.float32)
        tbl_24 = 0.05 * jax.random.normal(jax.random.fold_in(_tk, 500 + 24), (125000, 16), jnp.float32)
        tbl_25 = 0.05 * jax.random.normal(jax.random.fold_in(_tk, 500 + 25), (125000, 16), jnp.float32)
        tbl_26 = 0.05 * jax.random.normal(jax.random.fold_in(_tk, 500 + 26), (1000, 16), jnp.float32)
        tbl_27 = 0.05 * jax.random.normal(jax.random.fold_in(_tk, 500 + 27), (1000, 16), jnp.float32)
        tbl_28 = 0.05 * jax.random.normal(jax.random.fold_in(_tk, 500 + 28), (1250, 16), jnp.float32)
        tbl_29 = 0.05 * jax.random.normal(jax.random.fold_in(_tk, 500 + 29), (1000, 16), jnp.float32)
        tbl_30 = 0.05 * jax.random.normal(jax.random.fold_in(_tk, 500 + 30), (1000, 16), jnp.float32)
        tbl_31 = 0.05 * jax.random.normal(jax.random.fold_in(_tk, 500 + 31), (1250, 16), jnp.float32)
        _rk = jax.random.fold_in(_tk, 7)
        W_top1 = 0.0693375 * jax.random.normal(jax.random.fold_in(_tk, 801), (208, 512), jnp.float32)
        W_top2 = 0.0441942 * jax.random.normal(jax.random.fold_in(_tk, 802), (512, 256), jnp.float32)
        W_top3 = 0.0625 * jax.random.normal(jax.random.fold_in(_tk, 803), (256, 1), jnp.float32)
        b_top1 = jnp.zeros((512,), jnp.float32)
        b_top2 = jnp.zeros((256,), jnp.float32)
        return (dense_ctx, ids, tbl_0, tbl_1, tbl_2, tbl_3, tbl_4, tbl_5, tbl_6, tbl_7, tbl_8, tbl_9, tbl_10, tbl_11, tbl_12, tbl_13, tbl_14, tbl_15, tbl_16, tbl_17, tbl_18, tbl_19, tbl_20, tbl_21, tbl_22, tbl_23, tbl_24, tbl_25, tbl_26, tbl_27, tbl_28, tbl_29, tbl_30, tbl_31, W_top1, b_top1, W_top2, b_top2, W_top3)
    dense_ctx, ids, tbl_0, tbl_1, tbl_2, tbl_3, tbl_4, tbl_5, tbl_6, tbl_7, tbl_8, tbl_9, tbl_10, tbl_11, tbl_12, tbl_13, tbl_14, tbl_15, tbl_16, tbl_17, tbl_18, tbl_19, tbl_20, tbl_21, tbl_22, tbl_23, tbl_24, tbl_25, tbl_26, tbl_27, tbl_28, tbl_29, tbl_30, tbl_31, W_top1, b_top1, W_top2, b_top2, W_top3 = _rec_inputs()

    def _L0_rec_setup():
        import jax, jax.numpy as jnp
        import numpy as np
        B, M, D = (2048, 32, 16)
        LAYERS = [64, 64, 64]
        key = jax.random.key(seed)
        ks = jax.random.split(key, 4)
        inp = {'embeddings': jax.random.normal(ks[0], (B, M, D), dtype=jnp.float32)}
        hk_1 = M
        for i, hk in enumerate(LAYERS):
            scale = (2.0 / (M * hk_1 + hk)) ** 0.5
            inp[f'W{i}'] = jax.random.normal(ks[i + 1], (M, hk_1, hk), dtype=jnp.float32) * scale
            hk_1 = hk
        return inp
    _L0_rec_all = _L0_rec_setup()
    _L0_rec_in = {k: v for k, v in _L0_rec_all.items() if k in ('W0', 'W1', 'W2')}
    del _L0_rec_all
    return {'dense_ctx': dense_ctx, 'ids': ids, 'tbl_0': tbl_0, 'tbl_1': tbl_1, 'tbl_2': tbl_2, 'tbl_3': tbl_3, 'tbl_4': tbl_4, 'tbl_5': tbl_5, 'tbl_6': tbl_6, 'tbl_7': tbl_7, 'tbl_8': tbl_8, 'tbl_9': tbl_9, 'tbl_10': tbl_10, 'tbl_11': tbl_11, 'tbl_12': tbl_12, 'tbl_13': tbl_13, 'tbl_14': tbl_14, 'tbl_15': tbl_15, 'tbl_16': tbl_16, 'tbl_17': tbl_17, 'tbl_18': tbl_18, 'tbl_19': tbl_19, 'tbl_20': tbl_20, 'tbl_21': tbl_21, 'tbl_22': tbl_22, 'tbl_23': tbl_23, 'tbl_24': tbl_24, 'tbl_25': tbl_25, 'tbl_26': tbl_26, 'tbl_27': tbl_27, 'tbl_28': tbl_28, 'tbl_29': tbl_29, 'tbl_30': tbl_30, 'tbl_31': tbl_31, 'W_top1': W_top1, 'b_top1': b_top1, 'W_top2': W_top2, 'b_top2': b_top2, 'W_top3': W_top3, 'L0_rec_W0': _L0_rec_in['W0'], 'L0_rec_W1': _L0_rec_in['W1'], 'L0_rec_W2': _L0_rec_in['W2']}

def reference(dense_ctx, ids, tbl_0, tbl_1, tbl_2, tbl_3, tbl_4, tbl_5, tbl_6, tbl_7, tbl_8, tbl_9, tbl_10, tbl_11, tbl_12, tbl_13, tbl_14, tbl_15, tbl_16, tbl_17, tbl_18, tbl_19, tbl_20, tbl_21, tbl_22, tbl_23, tbl_24, tbl_25, tbl_26, tbl_27, tbl_28, tbl_29, tbl_30, tbl_31, W_top1, b_top1, W_top2, b_top2, W_top3, L0_rec_W0, L0_rec_W1, L0_rec_W2):
    import jax
    import jax.numpy as jnp

    def _L0_rec_ref(embeddings, W0, W1, W2):
        import jax, jax.numpy as jnp
        import numpy as np
        B, M, D = (2048, 32, 16)
        LAYERS = [64, 64, 64]
        x0 = embeddings
        xk = x0
        outs = []
        for W in (W0, W1, W2):
            xk = jax.nn.relu(jnp.einsum('bmd,bhd,mhk->bkd', x0, xk, W))
            outs.append(jnp.sum(xk, axis=2))
        return jnp.concatenate(outs, axis=1)
    e = jnp.stack([tbl_0[ids[:, 0]], tbl_1[ids[:, 1]], tbl_2[ids[:, 2]], tbl_3[ids[:, 3]], tbl_4[ids[:, 4]], tbl_5[ids[:, 5]], tbl_6[ids[:, 6]], tbl_7[ids[:, 7]], tbl_8[ids[:, 8]], tbl_9[ids[:, 9]], tbl_10[ids[:, 10]], tbl_11[ids[:, 11]], tbl_12[ids[:, 12]], tbl_13[ids[:, 13]], tbl_14[ids[:, 14]], tbl_15[ids[:, 15]], tbl_16[ids[:, 16]], tbl_17[ids[:, 17]], tbl_18[ids[:, 18]], tbl_19[ids[:, 19]], tbl_20[ids[:, 20]], tbl_21[ids[:, 21]], tbl_22[ids[:, 22]], tbl_23[ids[:, 23]], tbl_24[ids[:, 24]], tbl_25[ids[:, 25]], tbl_26[ids[:, 26]], tbl_27[ids[:, 27]], tbl_28[ids[:, 28]], tbl_29[ids[:, 29]], tbl_30[ids[:, 30]], tbl_31[ids[:, 31]]], axis=1)
    z = _L0_rec_ref(e, L0_rec_W0, L0_rec_W1, L0_rec_W2)
    z = z.reshape(z.shape[0], -1)
    h = jnp.concatenate([z, dense_ctx], axis=1)
    h = jnp.maximum(h @ W_top1 + b_top1, 0.0)
    h = jnp.maximum(h @ W_top2 + b_top2, 0.0)
    y = h @ W_top3
    return y

_drawn_inputs = setup_inputs


def setup_inputs(seed=0):
    import zlib

    import numpy as np

    out = dict(_drawn_inputs(seed))
    spreads = {'b_top1': (0.0, 2.0), 'b_top2': (0.0, 0.8)}
    factors = {'tbl_0': 8.0,
     'tbl_1': 8.0,
     'tbl_2': 8.0,
     'tbl_3': 8.0,
     'tbl_4': 8.0,
     'tbl_5': 8.0,
     'tbl_6': 8.0,
     'tbl_7': 8.0,
     'tbl_8': 8.0,
     'tbl_9': 8.0,
     'tbl_10': 8.0,
     'tbl_11': 8.0,
     'tbl_12': 8.0,
     'tbl_13': 8.0,
     'tbl_14': 8.0,
     'tbl_15': 8.0,
     'tbl_16': 8.0,
     'tbl_17': 8.0,
     'tbl_18': 8.0,
     'tbl_19': 8.0,
     'tbl_20': 8.0,
     'tbl_21': 8.0,
     'tbl_22': 8.0,
     'tbl_23': 8.0,
     'tbl_24': 8.0,
     'tbl_25': 8.0,
     'tbl_26': 8.0,
     'tbl_27': 8.0,
     'tbl_28': 8.0,
     'tbl_29': 8.0,
     'tbl_30': 8.0,
     'tbl_31': 8.0,
     'L0_rec_W0': 3.468,
     'L0_rec_W1': 8.0,
     'L0_rec_W2': 8.0,
     'dense_ctx': 7.331}
    for name, (base, spread) in spreads.items():
        noise = np.random.default_rng([zlib.crc32(name.encode()), seed]).standard_normal(out[name].shape)
        drawn = base * np.exp(spread * noise) if base else spread * noise
        out[name] = jnp.asarray(drawn.astype(out[name].dtype))
    for name, factor in factors.items():
        out[name] = (out[name] * factor).astype(out[name].dtype)
    return out
```

```python
from contextlib import ExitStack

import concourse.bass as bass
from concourse import mybir

B, M, D, K = 512, 32, 16, 64
P = 128
NCH = B // P
GRP = 512
PAIR = 2 * GRP
COLS = P * D
NT0 = (M // 2 + 1 + 3) // 4
NT = M * K // P
TG = 4
NG = NT // TG
H1, H2 = 512, 256

RING_V = 4
RING_G = 2

PHASES = [(1, 0), (1, 1), (2, 0), (2, 1), (0, 0), (0, 1)]
LAST = PHASES[:4]
FIRST = [(0, 0), (0, 1)]
POOL_TILES = {(1, 0): (4, 8, 12), (1, 1): (4, 8, 12), (2, 0): (3, 6, 9, 12, 14), (2, 1): (3, 6, 9, 12, 14)}
STEP_SPLIT1 = ((2, 0), 1)
STEP_SPLIT2 = ((2, 0), 3)
STEP_TURN = ((2, 0), 5)
STEP_SPREAD = ((2, 0), 8)
STEP_SPREAD2 = ((2, 0), 10)
GATHERS = {(1, 0): 16, (1, 1): 16}


def tiles_of(phase):
    return NT0 if phase[0] == 0 else NT


def by_pool(phase, t):
    return t in POOL_TILES.get(phase, ())


class Counts:

    def __init__(self, phases):
        self.vector, self.pool = {}, {}
        v = g = 0
        for ph in phases:
            for t in range(tiles_of(ph)):
                self.vector[ph, t], self.pool[ph, t] = v, g
                if by_pool(ph, t):
                    g += 1
                else:
                    v += 1
        self.vector_total, self.pool_total = v, g

    def vector_after(self, ph, t):
        return self.vector[ph, t] + (not by_pool(ph, t))

    def pool_after(self, ph, t):
        return self.pool[ph, t] + by_pool(ph, t)


START, BODY = Counts(FIRST), Counts(PHASES)
V0, VN = START.vector_total, BODY.vector_total
GN = BODY.pool_total
Q0, QN = 2 * NT0, 2 * NT0
X0, XN = 2, 4
A0, AN = 2, 6


def v_slot_before(k):
    if k >= RING_V:
        return k - RING_V
    return max(-1 - (n - 1 - k) % RING_V for n in (START.vector_total, BODY.vector_total))


def cin_tower(nc, ids, tables, spread, w0_mh, w0_hm, w1, w2, w_top1, b_top1, w_top2, b_top2,
              w_top3, dense_t, out):
    f32, bf16, i32 = mybir.dt.float32, mybir.dt.bfloat16, mybir.dt.int32
    ALU, ACT, AX = mybir.AluOpType, mybir.ActivationFunctionType, mybir.AxisListType
    ctx = ExitStack()
    with ctx:
        def sb(name, shape, dt=f32):
            return ctx.enter_context(nc.sbuf_tensor(name, shape, dt))

        def ps(name, shape, dt=f32):
            return ctx.enter_context(nc.psum_tensor(name, shape, dt))

        def sem(name):
            return ctx.enter_context(nc.semaphore(name))

        x0_dram = nc.dram_tensor("x0_dram", (NCH, M, COLS), f32, kind="Internal").ap()

        x0b = sb("x0b", [P, 2, NT, PAIR])
        w1_sb = sb("w1_sb", [P, NT, K])
        w2_sb = sb("w2_sb", [P, NT, K])
        w0_sb = sb("w0_sb", [P, NT0, K])
        w0_add = sb("w0_add", [P, NT0, K])
        spread_sb = sb("spread_sb", [P, NT0 + 2, P], bf16)
        ids_all = sb("ids_all", [P, NCH, M], i32)
        ids_sb = sb("ids_sb", [P, M], i32)
        rows = sb("rows", [P, M, D])
        parts = sb("parts", [P, D, 4, M], bf16)
        parts_t = sb("parts_t", [P, COLS], bf16)
        x0_rep = sb("x0_rep", [P, COLS])
        x_pool = sb("x_pool", [P, 2, PAIR])
        z_v = sb("z_v", [P, RING_V, PAIR])
        z_g = sb("z_g", [P, RING_G, PAIR])
        act_sb = sb("act_sb", [P, 2, GRP])
        d_sums = sb("d_sums", [P, 3, B])
        d_part = sb("d_part", [P, P])
        b1_sb = sb("b1_sb", [P, H1 // P])
        b2_sb = sb("b2_sb", [P, H2 // P])
        late = x0b[:, 0, :, :].rearrange("p t c -> p (t c)")
        wt1_z = late[:, 0:3 * H1].rearrange("p (l n) -> p l n", l=3)
        wt1_d = late[0:D, 2048:2048 + H1]
        dense_sb = late[0:D, 2560:2560 + B]
        wt2 = late[:, 3072:4096].rearrange("p (t n) -> p t n", n=H2)
        wt3 = late[:, 4096:4098]
        h1 = late[:, 5120:5120 + H1 // P * B].rearrange("p (t c) -> p t c", c=B)
        h2 = late[:, 7168:7168 + H2 // P * B].rearrange("p (t c) -> p t c", c=B)
        y_sb = late[0:1, 8192:8192 + B]

        acc = ps("acc", [P, 2, GRP])
        x_ps = ps("x_ps", [P, 2, PAIR])
        q_ps = ps("q_ps", [P, PAIR])
        turned = q_ps[:, :].bitcast(bf16)

        ids_in = sem("ids_in")
        ids_ready = sem("ids_ready")
        consts_in = sem("consts_in")
        w0_in = sem("w0_in")
        w1_in = sem("w1_in")
        w2_in = sem("w2_in")
        top_in = sem("top_in")
        zero_done = sem("zero_done")
        w0_ready = sem("w0_ready")
        gathered = sem("gathered")
        part0_done = sem("part0_done")
        rest1_done = sem("rest1_done")
        part1_done = sem("part1_done")
        split_done = sem("split_done")
        turn_done = sem("turn_done")
        parts_t_done = sem("parts_t_done")
        spread_done = sem("spread_done")
        x0_rep_done = sem("x0_rep_done")
        x0_stored = sem("x0_stored")
        x0b_in = [[sem(f"x0b_in_{p}_{g}") for g in range(NG)] for p in range(2)]
        q_ready = sem("q_ready")
        z_v_made = sem("z_v_made")
        z_g_made = sem("z_g_made")
        z_v_used = sem("z_v_used")
        z_g_free = sem("z_g_free")
        x_ps_done = sem("x_ps_done")
        x_pool_done = sem("x_pool_done")
        acc_read = sem("acc_read")
        d_sum_done = sem("d_sum_done")
        d_part_done = sem("d_part_done")
        mlp_mm = sem("mlp_mm")
        mlp_act = sem("mlp_act")
        y_done = sem("y_done")
        y_out = sem("y_out")
        sp_step = sem("sp_step")
        pool_step = sem("pool_step")

        def q_buffer(pair, j):
            return q_ps[:, :] if (j + pair) % 2 == 0 else x_ps[:, pair, :]

        block = ctx.enter_context(nc.Block())

        @block.sync
        def _(sp):
            def x0_round_trip(c, first):
                sp.wait_ge(x0_rep_done, 2 * (c + 1))
                sp.sem_inc(sp_step, 1)
                sp.dma_start(x0_dram[c], x0_rep[0:M, :]).then_inc(x0_stored, 16)
                sp.wait_ge(x0_stored, 16 * (c + 1))
                sp.sem_inc(sp_step, 1)
                for p in range(2):
                    for g in range(NG):
                        if not first:
                            t = TG * g + TG - 1
                            sp.wait_ge(z_v_made, V0 + (c - 1) * VN + BODY.vector_after((2, p), t))
                            sp.sem_inc(sp_step, 1)
                            sp.wait_ge(z_g_made, (c - 1) * GN + BODY.pool_after((2, p), t))
                            sp.sem_inc(sp_step, 1)
                        for i in range(TG):
                            t = TG * g + i
                            src = x0_dram[c, 2 * t:2 * t + 2, p * PAIR:(p + 1) * PAIR]
                            src = src.rearrange("m (o n) -> m o n", o=1).to_broadcast([2, K, PAIR])
                            sp.dma_start(x0b[:, p, t, :], src).then_inc(x0b_in[p][g], 16)

            sp.dma_start(ids_all[:, :, :], ids.rearrange("(c p) f -> p c f", p=P)).then_inc(ids_in, 16)
            x0_round_trip(0, True)
            with sp.Fori(0, NCH - 1) as c:
                x0_round_trip(c + 1, False)

            sp.wait_ge(z_v_made, V0 + (NCH - 1) * VN + BODY.vector_after((2, 0), NT - 1))
            sp.wait_ge(z_g_made, (NCH - 1) * GN + BODY.pool_after((2, 0), NT - 1))
            z_rows = w_top1[0:3 * K, :].rearrange("(l k) n -> k l n", k=K)
            sp.dma_start(wt1_z[0:K, :, :], z_rows).then_inc(top_in, 16)
            sp.dma_start(wt1_z[K:P, :, :], z_rows).then_inc(top_in, 16)
            sp.dma_start(wt1_d, w_top1[3 * K:3 * K + D, :]).then_inc(top_in, 16)
            sp.dma_start(dense_sb, dense_t).then_inc(top_in, 16)
            sp.dma_start(wt2, w_top2.rearrange("(t p) n -> p t n", p=P)).then_inc(top_in, 16)
            sp.dma_start(wt3, w_top3).then_inc(top_in, 16)
            sp.wait_ge(y_done, 1)
            sp.dma_start(out.rearrange("b o -> o b"), y_sb).then_inc(y_out, 16)
            sp.wait_ge(y_out, 16)

        @block.gpsimd
        def _(pool):
            def gather(f):
                pool.indirect_dma_start(rows[:, f, :], None, tables[f],
                                        bass.IndirectOffsetOnAxis(ids_sb[:, f:f + 1], 0)).then_inc(gathered, 16)

            pool.wait_ge(ids_in, 16)
            pool.tensor_copy(ids_sb[:, :], ids_all[:, 0, :]).then_inc(ids_ready, 1)
            pool.wait_ge(ids_ready, 1)
            for f in range(M):
                gather(f)

            def turn(c, phases, next_chunk):
                f = 0
                if next_chunk:
                    pool.wait_ge(gathered, 16 * M * (c + 1))
                    pool.tensor_copy(ids_sb[:, :], ids_all[:, bass.ds(c + 1, 1), :].rearrange("p c f -> p (c f)")).then_inc(ids_ready, 1)
                    pool.wait_ge(ids_ready, c + 2)
                    pool.sem_inc(pool_step, 1)
                    pool.wait_ge(split_done, c + 1)
                    pool.sem_inc(pool_step, 1)
                for ph in phases:
                    layer, p = ph
                    mine = POOL_TILES.get(ph, ())
                    want = GATHERS.get(ph, 0) if next_chunk else 0
                    for n, t in enumerate(mine):
                        for _ in range(want * n // len(mine), want * (n + 1) // len(mine)):
                            gather(f)
                            f += 1
                        if n == 0:
                            pool.wait_ge(x_pool_done, c * XN + 2 * (layer - 1) + p + 1)
                        pool.wait_ge(x0b_in[p][t // TG], 16 * TG * (c + 1))
                        k = BODY.pool[ph, t]
                        pool.wait_ge(z_g_free, c * GN + k + 1)
                        pool.tensor_tensor(z_g[:, k % RING_G, :], x_pool[:, p, :], x0b[:, p, t, :],
                                           ALU.mult).then_inc(z_g_made, 1)

            with pool.Fori(0, NCH - 1) as c:
                turn(c, PHASES, True)
            turn(NCH - 1, LAST, False)

        @block.scalar
        def _(act):
            act.dma_start(spread_sb[:, :, :], spread.rearrange("t k p -> k t p")).then_inc(consts_in, 16)
            n = (NT0 - 1) * P
            for dst, src in ((w0_sb, w0_mh), (w0_add, w0_hm)):
                act.wait_ge(zero_done, 3)
                act.dma_start(dst[:, 0:NT0 - 1, :], src[0:n, :].rearrange("(t p) k -> p t k", p=P)).then_inc(w0_in, 16)
                act.dma_start(dst[0:M // 2, NT0 - 1, :], src[n:n + M // 2, :]).then_inc(w0_in, 16)
            act.dma_start(w1_sb[:, :, :], w1.rearrange("(t p) k -> p t k", p=P)).then_inc(w1_in, 16)
            act.dma_start(w2_sb[:, :, :], w2.rearrange("(t p) k -> p t k", p=P)).then_inc(w2_in, 16)
            act.dma_start(b1_sb[:, :], b_top1).then_inc(consts_in, 16)
            act.dma_start(b2_sb[:, :], b_top2).then_inc(consts_in, 16)

            def prepare(c):
                def part0():
                    act.wait_ge(gathered, 16 * M * (c + 1))
                    act.activation(parts[:, :, 0, :].rearrange("p d m -> p m d"), rows[:, :, :],
                                   ACT.Copy).then_inc(part0_done, 1)

                def part1():
                    act.wait_ge(rest1_done, c + 1)
                    act.activation(parts[:, :, 1, :].rearrange("p d m -> p m d"), rows[:, :, :],
                                   ACT.Copy).then_inc(part1_done, 1)

                def turn():
                    act.wait_ge(turn_done, c + 1)
                    act.activation(parts_t[:, :], turned, ACT.Copy).then_inc(parts_t_done, 1)

                def spread_half(h):
                    act.wait_ge(spread_done, 2 * c + h + 1)
                    act.activation(x0_rep[:, h * PAIR:(h + 1) * PAIR], q_ps[:, :],
                                   ACT.Copy).then_inc(x0_rep_done, 1)

                return part0, part1, turn, lambda: spread_half(0), lambda: spread_half(1)

            def evict(ph, base, n_read):
                layer, p = ph
                act.wait_ge(z_v_used, base + BODY.vector_after(ph, tiles_of(ph) - 1))
                if layer < 2:
                    for dst, done in ((x_ps, x_ps_done), (x_pool, x_pool_done)):
                        for grp in range(2):
                            for half in range(2):
                                last = act.activation(
                                    dst[half * K:(half + 1) * K, p, grp * GRP:(grp + 1) * GRP],
                                    acc[grp * K:(grp + 1) * K, p, :], ACT.Relu)
                        last.then_inc(done, 1)
                act.wait_ge(d_sum_done, n_read)
                act.activation(act_sb[:, p, :], acc[:, p, :], ACT.Relu).then_inc(acc_read, 1)

            def evict_first(ph):
                _, p = ph
                act.wait_ge(z_v_used, START.vector_after(ph, NT0 - 1))
                for dst, done in ((x_ps, x_ps_done), (x_pool, x_pool_done)):
                    for grp in range(2):
                        for half in range(2):
                            last = act.activation(
                                dst[half * K:(half + 1) * K, p, grp * GRP:(grp + 1) * GRP],
                                acc[grp * K:(grp + 1) * K, p, :], ACT.Relu)
                    last.then_inc(done, 1)
                act.activation(act_sb[:, p, :], acc[:, p, :], ACT.Relu).then_inc(acc_read, 1)

            for step in prepare(0):
                step()
            evict_first((0, 0))
            evict_first((0, 1))

            def turn(c, phases, next_chunk):
                steps = list(prepare(c + 1)) if next_chunk else []
                for i, ph in enumerate(phases):
                    evict(ph, V0 + c * VN, A0 + c * AN + i - 1)
                    if ph == (1, 1):
                        for step in steps:
                            step()

            with act.Fori(0, NCH - 1) as c:
                turn(c, PHASES, True)
            turn(NCH - 1, LAST, False)

            act.wait_ge(consts_in, 48)
            for n in range(H1 // P):
                act.wait_ge(mlp_mm, n + 1)
                act.activation(h1[:, n, :], x_ps[:, n // 2, (n % 2) * GRP:(n % 2 + 1) * GRP], ACT.Relu,
                               bias=b1_sb[:, n:n + 1]).then_inc(mlp_act, 1)
            for n in range(H2 // P):
                act.wait_ge(mlp_mm, H1 // P + n + 1)
                act.activation(h2[:, n, :], q_ps[:, n * GRP:(n + 1) * GRP], ACT.Relu,
                               bias=b2_sb[:, n:n + 1]).then_inc(mlp_act, 1)
            act.wait_ge(mlp_mm, (H1 + H2) // P + 1)
            act.activation(y_sb, acc[0:1, 0, :], ACT.Copy).then_inc(y_done, 1)

        @block.vector
        def _(dve):
            dve.memset(parts[:, :, 3, :], 0.0).then_inc(zero_done, 1)
            dve.memset(w0_sb[:, NT0 - 1, :], 0.0).then_inc(zero_done, 1)
            dve.memset(w0_add[:, NT0 - 1, :], 0.0).then_inc(zero_done, 1)
            dve.wait_ge(w0_in, 64)
            dve.tensor_tensor(w0_sb[:, :, :], w0_sb[:, :, :], w0_add[:, :, :], ALU.add).then_inc(w0_ready, 1)
            dve.wait_ge(w0_ready, 1)
            dve.tensor_scalar(w0_sb[0:M, 0, :], w0_sb[0:M, 0, :], 0.5, None, ALU.mult).then_inc(w0_ready, 1)

            def split1(c):
                dve.wait_ge(part0_done, c + 1)
                dve.tensor_tensor(rows[:, :, :], rows[:, :, :], parts[:, :, 0, :].rearrange("p d m -> p m d"),
                                  ALU.subtract).then_inc(rest1_done, 1)

            def split2(c):
                dve.wait_ge(part1_done, c + 1)
                dve.tensor_tensor(parts[:, :, 2, :].rearrange("p d m -> p m d"), rows[:, :, :],
                                  parts[:, :, 1, :].rearrange("p d m -> p m d"),
                                  ALU.subtract).then_inc(split_done, 1)

            def products(ph, c, base, q_base, count, hooks=None):
                layer, p = ph
                for t in range(tiles_of(ph)):
                    for at, step in (hooks or ()):
                        if at == (ph, t):
                            step()
                    if by_pool(ph, t):
                        continue
                    k = count.vector[ph, t]
                    if layer == 0:
                        dve.wait_ge(q_ready, q_base + NT0 * p + t + 1)
                        if t == 0:
                            dve.wait_ge(x0_rep_done, 2 * c + p + 1)
                        in0, in1 = q_buffer(p, t), x0_rep[:, p * PAIR:(p + 1) * PAIR]
                    else:
                        if t == 0:
                            dve.wait_ge(x_ps_done, c * XN + 2 * (layer - 1) + p + 1)
                        dve.wait_ge(x0b_in[p][t // TG], 16 * TG * (c + 1))
                        in0, in1 = x_ps[:, p, :], x0b[:, p, t, :]
                    if count is BODY or k >= RING_V:
                        dve.wait_ge(z_v_used, base + 1 + v_slot_before(k))
                    dve.tensor_tensor(z_v[:, k % RING_V, :], in0, in1, ALU.mult).then_inc(z_v_made, 1)

            def sums(ph, c, n, n_pairs):
                layer, p = ph
                dve.wait_ge(acc_read, n + 1)
                src = act_sb[:, p, :].rearrange("p (d b) -> p b d", b=P)
                if p == 0:
                    dve.tensor_reduce(d_sums[:, layer, bass.ds(c * P, P)], src, AX.X, ALU.add).then_inc(d_sum_done, 1)
                else:
                    if not (isinstance(n_pairs, int) and n_pairs == 0):
                        dve.wait_ge(d_part_done, n_pairs)
                    dve.tensor_reduce(d_part[:, :], src, AX.X, ALU.add).then_inc(d_sum_done, 1)
                    dve.wait_ge(d_sum_done, n + 1)
                    dst = d_sums[:, layer, bass.ds(c * P, P)]
                    dve.tensor_tensor(dst, dst, d_part[:, :], ALU.add).then_inc(d_part_done, 1)

            split1(0)
            split2(0)
            products((0, 0), 0, 0, 0, START)
            products((0, 1), 0, 0, 0, START)

            def turn(c, phases, next_chunk):
                base = V0 + c * VN
                hooks = ((STEP_SPLIT1, lambda: split1(c + 1)), (STEP_SPLIT2, lambda: split2(c + 1))) if next_chunk else ()
                before = {(1, 0): ((0, 0), c), (1, 1): ((0, 1), c), (2, 0): ((1, 0), c), (2, 1): ((1, 1), c),
                          (0, 0): ((2, 0), c), (0, 1): ((2, 1), c)}
                for i, ph in enumerate(phases):
                    done, chunk = before[ph]
                    nxt = c + 1 if ph[0] == 0 else c
                    products(ph, nxt, base, Q0 + c * QN, BODY, hooks)
                    sums(done, chunk, A0 + c * AN + i - 2, c * (AN // 2) + i // 2)

            with dve.Fori(0, NCH - 1) as c:
                turn(c, PHASES, True)
            turn(NCH - 1, LAST, False)
            last = A0 + (NCH - 1) * AN + 4
            sums((2, 0), NCH - 1, last - 2, last // 2 - 1)
            sums((2, 1), NCH - 1, last - 1, last // 2 - 1)

        @block.tensor
        def _(pe):
            pe.wait_ge(consts_in, 48)
            pe.wait_ge(zero_done, 3)
            ident = spread_sb[:, NT0 + 1, :]
            pe.sem_inc(z_g_free, RING_G)

            def turn_parts(c):
                pe.wait_ge(split_done, c + 1)
                for d in range(D):
                    last = pe.transpose(turned[:, d * P:(d + 1) * P], parts[:, d, :, :].rearrange("p k m -> p (k m)"), ident)
                last.then_inc(turn_done, 1)

            def spread_rep(c, h):
                if h == 0:
                    pe.wait_ge(parts_t_done, c + 1)
                else:
                    pe.wait_ge(x0_rep_done, 2 * c + 1)
                for n in range(2):
                    cols = slice(h * PAIR + n * GRP, h * PAIR + (n + 1) * GRP)
                    last = pe.matmul(q_ps[:, n * GRP:(n + 1) * GRP], spread_sb[:, NT0, :], parts_t[:, cols],
                                     start=True, stop=True)
                last.then_inc(spread_done, 1)

            def spread_q(p, j):
                buf = q_buffer(p, j)
                for n in range(2):
                    cols = slice(p * PAIR + n * GRP, p * PAIR + (n + 1) * GRP)
                    last = pe.matmul(buf[:, n * GRP:(n + 1) * GRP], spread_sb[:, j, :], parts_t[:, cols],
                                     start=True, stop=True)
                last.then_inc(q_ready, 1)

            def contract(ph, t, base, g_base, count):
                layer, p = ph
                if by_pool(ph, t):
                    k = count.pool[ph, t]
                    pe.wait_ge(z_g_made, g_base + k + 1)
                    z, used = z_g[:, k % RING_G, :], z_g_free
                else:
                    k = count.vector[ph, t]
                    pe.wait_ge(z_v_made, base + k + 1)
                    z, used = z_v[:, k % RING_V, :], z_v_used
                w = (w0_sb, w1_sb, w2_sb)[layer]
                for grp in range(2):
                    last = pe.matmul(acc[grp * K:(grp + 1) * K, p, :], w[:, t, :], z[:, grp * GRP:(grp + 1) * GRP],
                                     start=(t == 0), stop=(t == tiles_of(ph) - 1))
                last.then_inc(used, 1)

            def layer0(ph, base, count, q_next):
                _, p = ph
                for t in range(NT0):
                    k = count.vector[ph, t]
                    pe.wait_ge(z_v_made, base + k + 1)
                    if t + 2 < NT0:
                        spread_q(p, t + 2)
                    elif t + 2 == NT0 and p == 0:
                        spread_q(1, 0)
                    elif p == 0:
                        spread_q(1, 1)
                    contract(ph, t, base, 0, count)

            def run(phases, c, base, g_base, a_base, count, hooks):
                for i, ph in enumerate(phases):
                    if a_base is not None or i >= 2:
                        pe.wait_ge(acc_read, a_base + i - 1)
                    if ph[0] == 0:
                        layer0(ph, base, count, None)
                    else:
                        for t in range(NT):
                            for at, step in hooks:
                                if at == (ph, t):
                                    step()
                            contract(ph, t, base, g_base, count)

            turn_parts(0)
            spread_rep(0, 0)
            spread_rep(0, 1)
            pe.wait_ge(w0_ready, 2)
            pe.wait_ge(x0_rep_done, 2)
            spread_q(0, 0)
            spread_q(0, 1)
            run(FIRST, 0, 0, 0, None, START, ())
            pe.wait_ge(w1_in, 16)
            pe.wait_ge(w2_in, 16)

            def turn(c, phases, next_chunk):
                hooks = ()
                if next_chunk:
                    def first_q():
                        pe.wait_ge(x0_rep_done, 2 * (c + 2))
                        spread_q(0, 0)
                        spread_q(0, 1)
                    hooks = ((STEP_TURN, lambda: turn_parts(c + 1)), (STEP_SPREAD, lambda: spread_rep(c + 1, 0)),
                             (STEP_SPREAD2, lambda: spread_rep(c + 1, 1)), (((2, 1), NT - 6), first_q))
                run(phases, c, V0 + c * VN, c * GN, A0 + c * AN, BODY, hooks)

            with pe.Fori(0, NCH - 1) as c:
                turn(c, PHASES, True)
            turn(NCH - 1, LAST, False)

            n_acc = A0 + (NCH - 1) * AN + 4
            pe.wait_ge(acc_read, n_acc)
            pe.wait_ge(d_part_done, 3 * NCH)
            pe.wait_ge(top_in, 96)
            for n in range(H1 // P):
                dst = x_ps[:, n // 2, (n % 2) * GRP:(n % 2 + 1) * GRP]
                for l in range(3):
                    pe.matmul(dst, wt1_z[:, l, n * P:(n + 1) * P], d_sums[:, l, :], start=(l == 0), stop=False)
                pe.matmul(dst, wt1_d[:, n * P:(n + 1) * P], dense_sb, start=False, stop=True).then_inc(mlp_mm, 1)
            for n in range(H2 // P):
                for t in range(H1 // P):
                    pe.wait_ge(mlp_act, t + 1)
                    last = pe.matmul(q_ps[:, n * GRP:(n + 1) * GRP], wt2[:, t, n * P:(n + 1) * P], h1[:, t, :],
                                     start=(t == 0), stop=(t == H1 // P - 1))
                last.then_inc(mlp_mm, 1)
            for t in range(H2 // P):
                pe.wait_ge(mlp_act, H1 // P + t + 1)
                last = pe.matmul(acc[0:1, 0, :], wt3[:, t:t + 1], h2[:, t, :], start=(t == 0), stop=(t == H2 // P - 1))
            last.then_inc(mlp_mm, 1)


def kernel(**inputs):
    import ml_dtypes
    import numpy as np
    import concourse.bacc as bacc
    from concourse.bass_utils import run_bass_kernel_spmd

    nc = bacc.Bacc("TRN2", target_bir_lowering=False, num_devices=1)
    arrays = {}

    def give(name, a):
        a = np.ascontiguousarray(a)
        arrays[name] = a
        return nc.dram_tensor(name, a.shape, mybir.dt.from_np(a.dtype), kind="ExternalInput").ap()

    row = np.arange(P)
    fields = [(row + 4 * j + row // M) % M for j in range(NT0)] + [row % M]
    part_field = np.arange(P) % M
    spread = np.stack([part_field[:, None] == f[None, :] for f in fields] + [np.eye(P, dtype=bool)])
    spread = spread.astype(ml_dtypes.bfloat16)
    pairs = np.arange(M * (M // 2) + M // 2)
    m, h = pairs % M, (pairs % M + pairs // M) % M
    w0 = np.asarray(inputs["L0_rec_W0"])

    args = [
        give("ids", np.asarray(inputs["ids"])),
        [give(f"tbl_{f}", np.asarray(inputs[f"tbl_{f}"])) for f in range(M)],
        give("spread", spread),
        give("w0_mh", w0[m, h]),
        give("w0_hm", w0[h, m]),
        give("w1", np.asarray(inputs["L0_rec_W1"]).reshape(M * K, K)),
        give("w2", np.asarray(inputs["L0_rec_W2"]).reshape(M * K, K)),
        give("w_top1", np.asarray(inputs["W_top1"])),
        give("b_top1", np.asarray(inputs["b_top1"]).reshape(-1, P).T),
        give("w_top2", np.asarray(inputs["W_top2"])),
        give("b_top2", np.asarray(inputs["b_top2"]).reshape(-1, P).T),
        give("w_top3", np.asarray(inputs["W_top3"]).reshape(-1, P).T),
        give("dense_t", np.asarray(inputs["dense_ctx"]).T),
        nc.dram_tensor("y", (B, 1), mybir.dt.float32, kind="ExternalOutput").ap(),
    ]
    cin_tower(nc, *args)
    got = run_bass_kernel_spmd(nc, [arrays], core_ids=[0])
    return got.results[0]["y"]
```

```python
from contextlib import ExitStack

import concourse.bass as bass
from concourse import mybir

B, M, D, K = 512, 32, 16, 64
P = 128
NCH = B // P
GRP = 512
PAIR = 2 * GRP
COLS = P * D
NT0 = M // 2 // 4 + 1
NT = M * K // P
TG = 4
NG = NT // TG
H1, H2 = 512, 256

RING_V = 4
RING_G = 2
RING_A = 2

PHASES = [(1, 0), (1, 1), (2, 0), (2, 1)]
POOL_TILES = {(1, 0): (7, 13), (1, 1): (3, 7, 11, 14), (2, 0): (3, 7, 11, 14), (2, 1): (5, 11)}
POOL_TILES_LAST = {(1, 0): (2, 5, 8, 11, 14), (1, 1): (2, 5, 8, 11, 14), (2, 0): (2, 5, 8, 11, 14),
                   (2, 1): (3, 6, 9, 12, 14)}
GATHERS = {(2, 1): (5, 7), (1, 0): (7, 6), (1, 1): (4, 3, 0, 0), (2, 0): (0, 0, 0, 0)}
L0_PAIR0 = [((2, 1), t) for t in (0, 2, 4, 6, 8, 10)]
L0_PAIR1 = [((1, 0), t) for t in (0, 2, 4, 6, 8, 10)]
SPLIT1, SPLIT2 = ((1, 1), 11), ((1, 1), 14)
TURN, SPREAD0, SPREAD1 = ((2, 0), 3), ((2, 0), 9), ((2, 0), 11)
SUMS = {((1, 0), 5): (0, 0), ((1, 1), 3): (0, 1), ((1, 1), 7): (1, 0), ((2, 0), 6): (1, 1),
        ((2, 1), 6): (2, 0)}
SUM_BEFORE = ((1, 0), 3)


class Counts:

    def __init__(self, pool_tiles):
        self.pool_tiles = pool_tiles
        self.vector, self.pool = {}, {}
        v = g = 0
        for ph in PHASES:
            for t in range(NT):
                self.vector[ph, t], self.pool[ph, t] = v, g
                if self.by_pool(ph, t):
                    g += 1
                else:
                    v += 1
        self.vector_total, self.pool_total = v, g

    def by_pool(self, ph, t):
        return t in self.pool_tiles[ph]

    def vector_after(self, ph, t):
        return self.vector[ph, t] + (not self.by_pool(ph, t))

    def pool_after(self, ph, t):
        return self.pool[ph, t] + self.by_pool(ph, t)


BODY, END = Counts(POOL_TILES), Counts(POOL_TILES_LAST)
VN, GN = BODY.vector_total, BODY.pool_total
AN = 2 * NT0
assert VN % RING_V == 0 and GN % RING_G == 0 and AN % RING_A == 0
assert sum(map(sum, GATHERS.values())) == M


def cin_tower(nc, ids, tables, spread, w0, w0_t, w0_diag, w0_mh, w0_hm, w1, w2, w_top1, b_top1,
              w_top2, b_top2, w_top3, dense_t, out):
    f32, bf16, i32 = mybir.dt.float32, mybir.dt.bfloat16, mybir.dt.int32
    ALU, ACT, AX = mybir.AluOpType, mybir.ActivationFunctionType, mybir.AxisListType
    ctx = ExitStack()
    with ctx:
        def sb(name, shape, dt=f32):
            return ctx.enter_context(nc.sbuf_tensor(name, shape, dt))

        def ps(name, shape, dt=f32):
            return ctx.enter_context(nc.psum_tensor(name, shape, dt))

        def sem(name):
            return ctx.enter_context(nc.semaphore(name))

        x0_dram = nc.dram_tensor("x0_dram", (NCH, 2, M, PAIR), f32, kind="Internal").ap()

        x0b = sb("x0b", [P, 2, NT, PAIR])
        w1_sb = sb("w1_sb", [P, NT, K])
        w2_sb = sb("w2_sb", [P, NT, K])
        w0_sb = sb("w0_sb", [P, NT0, K])
        spread_sb = sb("spread_sb", [P, NT0 + 1, P], bf16)
        ids_all = sb("ids_all", [P, NCH, M], i32)
        ids_sb = sb("ids_sb", [P, M], i32)
        rows = sb("rows", [P, M, D])
        parts = sb("parts", [P, D, 4, M], bf16)
        parts_t = sb("parts_t", [P, COLS], bf16)
        x0_rows = sb("x0_rows", [2 * M, PAIR])
        x_pool = sb("x_pool", [P, 2, PAIR])
        z_v = sb("z_v", [P, RING_V, PAIR])
        z_g = sb("z_g", [P, RING_G, PAIR])
        z_a = sb("z_a", [P, RING_A, PAIR])
        act_sb = sb("act_sb", [P, 2, GRP])
        d_sums = sb("d_sums", [P, 3, B])
        d_part = sb("d_part", [P, P])
        b1_sb = sb("b1_sb", [P, H1 // P])
        b2_sb = sb("b2_sb", [P, H2 // P])
        early = x0b[:, 1, :, :].rearrange("p t c -> p (t c)")
        w0_all = early[0:M, 0:M * K]
        w0_all_t = early[0:M, M * K:2 * M * K]
        w0_sum = early[0:M, 2 * M * K:2 * M * K + K]
        w0_twice = early[0:M, 2 * M * K + K:2 * M * K + 2 * K]
        w0_add = early[:, 2 * M * K + 2 * K:2 * M * K + 2 * K + (NT0 - 1) * K].rearrange("p (t k) -> p t k", k=K)
        late = x0b[:, 0, :, :].rearrange("p t c -> p (t c)")
        wt1_z = late[:, 0:3 * H1].rearrange("p (l n) -> p l n", l=3)
        wt1_d = late[0:D, 2048:2048 + H1]
        dense_sb = late[0:D, 2560:2560 + B]
        wt2 = late[:, 3072:4096].rearrange("p (t n) -> p t n", n=H2)
        wt3 = late[:, 4096:4098]
        h1 = late[:, 5120:5120 + H1 // P * B].rearrange("p (t c) -> p t c", c=B)
        h2 = late[:, 7168:7168 + H2 // P * B].rearrange("p (t c) -> p t c", c=B)
        y_sb = late[0:1, 8192:8192 + B]

        acc = ps("acc", [P, 2, GRP])
        x_ps = ps("x_ps", [P, 2, PAIR])
        q_ps = ps("q_ps", [P, PAIR])
        turned = q_ps[:, :].bitcast(bf16)

        ids_in, ids_ready = sem("ids_in"), sem("ids_ready")
        consts_in, w0_in, w1_in, w2_in, top_in = (sem(n) for n in ("consts_in", "w0_in", "w1_in", "w2_in", "top_in"))
        zero_done, w0_step, w0_ready = sem("zero_done"), sem("w0_step"), sem("w0_ready")
        gathered = sem("gathered")
        part0_done, rest1_done, part1_done = sem("part0_done"), sem("rest1_done"), sem("part1_done")
        split_done = sem("split_done")
        turn_done, parts_t_done = sem("turn_done"), sem("parts_t_done")
        spread_done, x0_rows_done = sem("spread_done"), sem("x0_rows_done")
        x0_stored = [sem(f"x0_stored_{p}") for p in range(2)]
        x0b_in = [[sem(f"x0b_in_{p}_{g}") for g in range(NG)] for p in range(2)]
        q_ready = sem("q_ready")
        z_v_made, z_g_made, z_a_made = sem("z_v_made"), sem("z_g_made"), sem("z_a_made")
        z_v_free, z_g_free, z_a_free = sem("z_v_free"), sem("z_g_free"), sem("z_a_free")
        x_ps_done = [sem(f"x_ps_done_{p}") for p in range(2)]
        x_pool_done = [sem(f"x_pool_done_{p}") for p in range(2)]
        acts_out = [sem(f"acts_out_{p}") for p in range(2)]
        acts_free = [sem(f"acts_free_{p}") for p in range(2)]
        d_part_done = sem("d_part_done")
        mlp_mm, mlp_act, y_done, y_out = sem("mlp_mm"), sem("mlp_act"), sem("y_done"), sem("y_out")
        sp_step, pool_step = sem("sp_step"), sem("pool_step")

        def q_buffer(pair, j):
            return q_ps[:, :] if (pair * NT0 + j) % 2 == 0 else x_ps[:, pair, :]

        def steps_at(hooks, ph, t):
            for at, step in hooks:
                if at == (ph, t):
                    step()

        block = ctx.enter_context(nc.Block())

        @block.sync
        def _(sp):
            def x0_round_trip(c, first):
                for p in range(2):
                    sp.wait_ge(x0_rows_done, 2 * c + p + 1)
                    sp.sem_inc(sp_step, 1)
                    sp.dma_start(x0_dram[c, p], x0_rows[M * p:M * p + M, :]).then_inc(x0_stored[p], 16)
                for p in range(2):
                    sp.wait_ge(x0_stored[p], 16 * (c + 1))
                    sp.sem_inc(sp_step, 1)
                    if first and p == 1:
                        sp.wait_ge(w0_ready, 1)
                    for g in range(NG):
                        if not first:
                            t = TG * g + TG - 1
                            sp.wait_ge(z_v_made, (c - 1) * VN + BODY.vector_after((2, p), t))
                            sp.sem_inc(sp_step, 1)
                            sp.wait_ge(z_g_made, (c - 1) * GN + BODY.pool_after((2, p), t))
                            sp.sem_inc(sp_step, 1)
                        for t in range(TG * g, TG * (g + 1)):
                            src = x0_dram[c, p, 2 * t:2 * t + 2, :]
                            src = src.rearrange("m (o n) -> m o n", o=1).to_broadcast([2, K, PAIR])
                            sp.dma_start(x0b[:, p, t, :], src).then_inc(x0b_in[p][g], 16)

            sp.dma_start(ids_all[:, :, :], ids.rearrange("(c p) f -> p c f", p=P)).then_inc(ids_in, 16)
            x0_round_trip(0, True)
            with sp.Fori(0, NCH - 1) as c:
                x0_round_trip(c + 1, False)

            sp.wait_ge(z_v_made, (NCH - 1) * VN + END.vector_after((2, 0), NT - 1))
            sp.wait_ge(z_g_made, (NCH - 1) * GN + END.pool_after((2, 0), NT - 1))
            z_rows = w_top1[0:3 * K, :].rearrange("(l k) n -> k l n", k=K)
            sp.dma_start(wt1_z[0:K, :, :], z_rows).then_inc(top_in, 16)
            sp.dma_start(wt1_z[K:P, :, :], z_rows).then_inc(top_in, 16)
            sp.dma_start(wt1_d, w_top1[3 * K:3 * K + D, :]).then_inc(top_in, 16)
            sp.dma_start(dense_sb, dense_t).then_inc(top_in, 16)
            sp.dma_start(wt2, w_top2.rearrange("(t p) n -> p t n", p=P)).then_inc(top_in, 16)
            sp.dma_start(wt3, w_top3).then_inc(top_in, 16)
            sp.wait_ge(y_done, 1)
            sp.dma_start(out.rearrange("b o -> o b"), y_sb).then_inc(y_out, 16)
            sp.wait_ge(y_out, 16)

        @block.gpsimd
        def _(pool):
            def start_gathers(c):
                if isinstance(c, int) and c == 0:
                    pool.wait_ge(ids_in, 16)
                    pool.tensor_copy(ids_sb[:, :], ids_all[:, 0, :]).then_inc(ids_ready, 1)
                    pool.wait_ge(ids_ready, 1)
                    return
                pool.wait_ge(gathered, 16 * M * c)
                pool.tensor_copy(ids_sb[:, :], ids_all[:, bass.ds(c, 1), :].rearrange("p c f -> p (c f)"))\
                    .then_inc(ids_ready, 1)
                pool.wait_ge(ids_ready, c + 1)
                pool.sem_inc(pool_step, 1)
                pool.wait_ge(split_done, c)
                pool.sem_inc(pool_step, 1)

            def gather(f):
                pool.indirect_dma_start(rows[:, f, :], None, tables[f],
                                        bass.IndirectOffsetOnAxis(ids_sb[:, f:f + 1], 0)).then_inc(gathered, 16)

            def phase(ph, c, count, field):
                layer, p = ph
                for n, t in enumerate(count.pool_tiles[ph]):
                    if field is not None:
                        for _ in range(GATHERS[ph][n]):
                            gather(field)
                            field += 1
                    if n == 0:
                        pool.wait_ge(x_pool_done[p], 2 * c + layer)
                    pool.wait_ge(x0b_in[p][t // TG], 16 * TG * (c + 1))
                    k = count.pool[ph, t]
                    pool.wait_ge(z_g_free, c * GN + k + 1)
                    pool.tensor_tensor(z_g[:, k % RING_G, :], x_pool[:, p, :], x0b[:, p, t, :],
                                       ALU.mult).then_inc(z_g_made, 1)
                return field

            def from_layer1(c, count, field):
                for ph in PHASES[:3]:
                    field = phase(ph, c, count, field)

            start_gathers(0)
            for f in range(M):
                gather(f)
            start_gathers(1)
            early_fields = sum(GATHERS[2, 1])
            for f in range(early_fields):
                gather(f)
            from_layer1(0, BODY, early_fields)
            with pool.Fori(1, NCH - 1) as c:
                start_gathers(c + 1)
                field = phase((2, 1), c - 1, BODY, 0)
                from_layer1(c, BODY, field)
            phase((2, 1), NCH - 2, BODY, None)
            from_layer1(NCH - 1, END, None)
            phase((2, 1), NCH - 1, END, None)

        @block.scalar
        def _(act):
            act.dma_start(spread_sb[:, :, :], spread.rearrange("t k p -> k t p")).then_inc(consts_in, 16)
            act.dma_start(w0_sb[:, 0:NT0 - 1, :], w0_mh.rearrange("(t p) k -> p t k", p=P)).then_inc(w0_in, 16)
            act.dma_start(w0_add, w0_hm.rearrange("(t p) k -> p t k", p=P)).then_inc(w0_in, 16)
            act.dma_start(w0_all, w0.rearrange("m h k -> m (h k)")).then_inc(w0_in, 16)
            act.dma_start(w0_all_t, w0_t.rearrange("m h k -> m (h k)")).then_inc(w0_in, 16)
            act.dma_start(w0_twice, w0_diag).then_inc(w0_in, 16)
            act.dma_start(w1_sb[:, :, :], w1.rearrange("(t p) k -> p t k", p=P)).then_inc(w1_in, 16)
            act.dma_start(w2_sb[:, :, :], w2.rearrange("(t p) k -> p t k", p=P)).then_inc(w2_in, 16)
            act.dma_start(b1_sb[:, :], b_top1).then_inc(consts_in, 16)
            act.dma_start(b2_sb[:, :], b_top2).then_inc(consts_in, 16)

            def part0(c):
                act.wait_ge(gathered, 16 * M * (c + 1))
                act.activation(parts[:, :, 0, :].rearrange("p d m -> p m d"), rows[:, :, :],
                               ACT.Copy).then_inc(part0_done, 1)

            def part1(c):
                act.wait_ge(rest1_done, c + 1)
                act.activation(parts[:, :, 1, :].rearrange("p d m -> p m d"), rows[:, :, :],
                               ACT.Copy).then_inc(part1_done, 1)

            def turn(c):
                act.wait_ge(turn_done, c + 1)
                act.activation(parts_t[:, :], turned, ACT.Copy).then_inc(parts_t_done, 1)

            def spread_half(c, p):
                act.wait_ge(spread_done, 2 * c + p + 1)
                act.activation(x0_rows[M * p:M * p + M, :], q_ps[0:M, :], ACT.Copy).then_inc(x0_rows_done, 1)

            def squares(c, p):
                for t in range(NT0):
                    n = p * NT0 + t
                    act.wait_ge(q_ready, c * AN + n + 1)
                    act.wait_ge(z_a_free, c * AN + n + 1)
                    act.activation(z_a[:, n % RING_A, :], q_buffer(p, t), ACT.Square).then_inc(z_a_made, 1)

            def evict(layer, p, c, base=None, count=None):
                if layer == 0:
                    act.wait_ge(z_a_free, RING_A + c * AN + (p + 1) * NT0)
                else:
                    act.wait_ge(z_v_free, RING_V + c * VN + count.vector_after((layer, p), NT - 1))
                if layer < 2:
                    for dst, done in ((x_ps, x_ps_done[p]), (x_pool, x_pool_done[p])):
                        for grp in range(2):
                            for half in range(2):
                                last = act.activation(
                                    dst[half * K:(half + 1) * K, p, grp * GRP:(grp + 1) * GRP],
                                    acc[grp * K:(grp + 1) * K, p, :], ACT.Relu)
                        last.then_inc(done, 1)
                act.wait_ge(acts_free[p], 3 * c + layer + 1)
                act.activation(act_sb[:, p, :], acc[:, p, :], ACT.Relu).then_inc(acts_out[p], 1)

            act.sem_inc(acts_out[1], 1)
            part0(0)
            part1(0)
            turn(0)
            spread_half(0, 0)
            spread_half(0, 1)
            squares(0, 0)
            evict(0, 0, 0)

            def chunk(c, count, last):
                squares(c, 1)
                evict(0, 1, c)
                evict(1, 0, c, count=count)
                if not last:
                    part0(c + 1)
                    part1(c + 1)
                evict(1, 1, c, count=count)
                if not last:
                    turn(c + 1)
                    spread_half(c + 1, 0)
                    spread_half(c + 1, 1)
                evict(2, 0, c, count=count)
                if not last:
                    squares(c + 1, 0)
                    evict(0, 0, c + 1)
                evict(2, 1, c, count=count)

            with act.Fori(0, NCH - 1) as c:
                chunk(c, BODY, False)
            chunk(NCH - 1, END, True)

            act.wait_ge(consts_in, 48)
            for n in range(H1 // P):
                act.wait_ge(mlp_mm, n + 1)
                act.activation(h1[:, n, :], x_ps[:, n // 2, (n % 2) * GRP:(n % 2 + 1) * GRP], ACT.Relu,
                               bias=b1_sb[:, n:n + 1]).then_inc(mlp_act, 1)
            for n in range(H2 // P):
                act.wait_ge(mlp_mm, H1 // P + n + 1)
                act.activation(h2[:, n, :], q_ps[:, n * GRP:(n + 1) * GRP], ACT.Relu,
                               bias=b2_sb[:, n:n + 1]).then_inc(mlp_act, 1)
            act.wait_ge(mlp_mm, (H1 + H2) // P + 1)
            act.activation(y_sb, acc[0:1, 0, :], ACT.Copy).then_inc(y_done, 1)

        @block.vector
        def _(dve):
            dve.memset(parts[:, :, 3, :], 0.0).then_inc(zero_done, 1)
            dve.memset(w0_sb[:, NT0 - 1, :], 0.0).then_inc(zero_done, 1)
            for p in range(2):
                dve.sem_inc(acts_free[p], 1)
            dve.wait_ge(w0_in, 80)
            w0_pairs = w0_sb[:, 0:NT0 - 1, :]
            dve.tensor_tensor(w0_pairs, w0_pairs, w0_add, ALU.add).then_inc(w0_step, 1)
            dve.tensor_tensor(w0_all, w0_all, w0_all_t, ALU.add).then_inc(w0_step, 1)
            dve.wait_ge(w0_step, 2)
            dve.tensor_scalar(w0_pairs, w0_pairs, 0.5, None, ALU.mult).then_inc(w0_step, 1)
            dve.tensor_reduce(w0_sum, w0_all.rearrange("m (h k) -> m k h", k=K), AX.X, ALU.add).then_inc(w0_step, 1)
            dve.tensor_scalar(w0_twice, w0_twice, 2.0, None, ALU.mult).then_inc(w0_step, 1)
            dve.wait_ge(w0_step, 5)
            twice = w0_sb[P - M:P, NT0 - 2, :]
            dve.tensor_scalar(twice, twice, 0.5, None, ALU.mult).then_inc(w0_step, 1)
            dve.wait_ge(zero_done, 2)
            dve.scalar_tensor_tensor(w0_sb[0:M, NT0 - 1, :], w0_sum, -0.5, w0_twice, ALU.mult,
                                     ALU.add).then_inc(w0_step, 1)
            dve.wait_ge(w0_step, 7)
            dve.sem_inc(w0_ready, 1)

            def split1(c):
                dve.wait_ge(part0_done, c + 1)
                dve.tensor_tensor(rows[:, :, :], rows[:, :, :], parts[:, :, 0, :].rearrange("p d m -> p m d"),
                                  ALU.subtract).then_inc(rest1_done, 1)

            def split2(c):
                dve.wait_ge(part1_done, c + 1)
                dve.tensor_tensor(parts[:, :, 2, :].rearrange("p d m -> p m d"), rows[:, :, :],
                                  parts[:, :, 1, :].rearrange("p d m -> p m d"),
                                  ALU.subtract).then_inc(split_done, 1)

            def sums(layer, p, c):
                n = 3 * c + layer
                dve.wait_ge(acts_out[p], n + 1 + p)
                src = act_sb[:, p, :].rearrange("p (d b) -> p b d", b=P)
                dst = d_sums[:, layer, bass.ds(c * P, P)]
                if p == 0:
                    dve.tensor_reduce(dst, src, AX.X, ALU.add).then_inc(acts_free[p], 1)
                    return
                if not (isinstance(n, int) and n == 0):
                    dve.wait_ge(d_part_done, n)
                dve.tensor_reduce(d_part[:, :], src, AX.X, ALU.add).then_inc(acts_free[p], 1)
                dve.wait_ge(acts_free[p], n + 2)
                dve.tensor_tensor(dst, dst, d_part[:, :], ALU.add).then_inc(d_part_done, 1)

            def chunk(c, count, first, last):
                hooks = [(at, lambda lp=lp: sums(*lp, c)) for at, lp in SUMS.items()]
                if not first:
                    hooks.append((SUM_BEFORE, lambda: sums(2, 1, c - 1)))
                if not last:
                    hooks += [(SPLIT1, lambda: split1(c + 1)), (SPLIT2, lambda: split2(c + 1))]
                for ph in PHASES:
                    layer, p = ph
                    for t in range(NT):
                        steps_at(hooks, ph, t)
                        if count.by_pool(ph, t):
                            continue
                        k = count.vector[ph, t]
                        if t == 0:
                            dve.wait_ge(x_ps_done[p], 2 * c + layer)
                        if count.vector[ph, TG * (t // TG)] == k:
                            dve.wait_ge(x0b_in[p][t // TG], 16 * TG * (c + 1))
                        dve.wait_ge(z_v_free, c * VN + k + 1)
                        dve.tensor_tensor(z_v[:, k % RING_V, :], x_ps[:, p, :], x0b[:, p, t, :],
                                          ALU.mult).then_inc(z_v_made, 1)

            split1(0)
            split2(0)
            chunk(0, BODY, True, False)
            with dve.Fori(1, NCH - 1) as c:
                chunk(c, BODY, False, False)
            chunk(NCH - 1, END, False, True)
            sums(2, 1, NCH - 1)

        @block.tensor
        def _(pe):
            pe.wait_ge(consts_in, 48)
            pe.wait_ge(zero_done, 2)
            ident = spread_sb[:, NT0, :]
            pe.sem_inc(z_v_free, RING_V)
            pe.sem_inc(z_g_free, RING_G)
            pe.sem_inc(z_a_free, RING_A)

            def turn_parts(c):
                pe.wait_ge(split_done, c + 1)
                for d in range(D):
                    last = pe.transpose(turned[:, d * P:(d + 1) * P], parts[:, d, :, :].rearrange("p k m -> p (k m)"), ident)
                last.then_inc(turn_done, 1)

            def spread_to(dst, j, p):
                for n in range(2):
                    cols = slice(p * PAIR + n * GRP, p * PAIR + (n + 1) * GRP)
                    last = pe.matmul(dst[:, n * GRP:(n + 1) * GRP], spread_sb[:, j, :], parts_t[:, cols],
                                     start=True, stop=True)
                return last

            def spread_x0(c, p):
                if p == 0:
                    pe.wait_ge(parts_t_done, c + 1)
                else:
                    pe.wait_ge(x0_rows_done, 2 * c + 1)
                spread_to(q_ps[:, :], NT0 - 1, p).then_inc(spread_done, 1)

            def multiply(w, z, p, start, stop):
                for grp in range(2):
                    last = pe.matmul(acc[grp * K:(grp + 1) * K, p, :], w, z[:, grp * GRP:(grp + 1) * GRP],
                                     start=start, stop=stop)
                return last

            def layer0_steps(c, p):
                def first():
                    if p == 0:
                        pe.wait_ge(x0_rows_done, 2 * (c + 1))
                    else:
                        pe.wait_ge(z_a_made, c * AN + NT0)
                    for j in range(2):
                        spread_to(q_buffer(p, j), j, p).then_inc(q_ready, 1)
                    pe.wait_ge(acts_out[p], 3 * c + 1 if p else 3 * c)

                def tile(t):
                    n = p * NT0 + t
                    pe.wait_ge(z_a_made, c * AN + n + 1)
                    if t + 2 < NT0:
                        spread_to(q_buffer(p, t + 2), t + 2, p).then_inc(q_ready, 1)
                    multiply(w0_sb[:, t, :], z_a[:, n % RING_A, :], p, t == 0, t == NT0 - 1).then_inc(z_a_free, 1)

                return [first] + [lambda t=t: tile(t) for t in range(NT0)]

            def chunk(c, count, last):
                hooks = list(zip(L0_PAIR1, layer0_steps(c, 1)))
                if not last:
                    hooks += [(TURN, lambda: turn_parts(c + 1)), (SPREAD0, lambda: spread_x0(c + 1, 0)),
                              (SPREAD1, lambda: spread_x0(c + 1, 1))]
                    hooks += zip(L0_PAIR0, layer0_steps(c + 1, 0))
                for ph in PHASES:
                    layer, p = ph
                    w = (w1_sb, w2_sb)[layer - 1]
                    for t in range(NT):
                        steps_at(hooks, ph, t)
                        if t == 0:
                            pe.wait_ge(acts_out[p], 3 * c + layer + p)
                        if count.by_pool(ph, t):
                            k = count.pool[ph, t]
                            pe.wait_ge(z_g_made, c * GN + k + 1)
                            z, used = z_g[:, k % RING_G, :], z_g_free
                        else:
                            k = count.vector[ph, t]
                            pe.wait_ge(z_v_made, c * VN + k + 1)
                            z, used = z_v[:, k % RING_V, :], z_v_free
                        multiply(w[:, t, :], z, p, t == 0, t == NT - 1).then_inc(used, 1)

            turn_parts(0)
            spread_x0(0, 0)
            spread_x0(0, 1)
            pe.wait_ge(w0_ready, 1)
            pe.wait_ge(x0_rows_done, 2)
            for j in range(2):
                spread_to(q_buffer(0, j), j, 0).then_inc(q_ready, 1)
            for step in layer0_steps(0, 0)[1:]:
                step()
            pe.wait_ge(w1_in, 16)
            pe.wait_ge(w2_in, 16)
            with pe.Fori(0, NCH - 1) as c:
                chunk(c, BODY, False)
            chunk(NCH - 1, END, True)

            pe.wait_ge(acts_out[0], 3 * NCH)
            pe.wait_ge(d_part_done, 3 * NCH)
            pe.wait_ge(top_in, 96)
            for n in range(H1 // P):
                dst = x_ps[:, n // 2, (n % 2) * GRP:(n % 2 + 1) * GRP]
                for l in range(3):
                    pe.matmul(dst, wt1_z[:, l, n * P:(n + 1) * P], d_sums[:, l, :], start=(l == 0), stop=False)
                pe.matmul(dst, wt1_d[:, n * P:(n + 1) * P], dense_sb, start=False, stop=True).then_inc(mlp_mm, 1)
            for n in range(H2 // P):
                for t in range(H1 // P):
                    pe.wait_ge(mlp_act, t + 1)
                    last = pe.matmul(q_ps[:, n * GRP:(n + 1) * GRP], wt2[:, t, n * P:(n + 1) * P], h1[:, t, :],
                                     start=(t == 0), stop=(t == H1 // P - 1))
                last.then_inc(mlp_mm, 1)
            for t in range(H2 // P):
                pe.wait_ge(mlp_act, H1 // P + t + 1)
                last = pe.matmul(acc[0:1, 0, :], wt3[:, t:t + 1], h2[:, t, :], start=(t == 0), stop=(t == H2 // P - 1))
            last.then_inc(mlp_mm, 1)


def kernel(**inputs):
    import ml_dtypes
    import numpy as np
    import concourse.bacc as bacc
    from concourse.bass_utils import run_bass_kernel_spmd

    nc = bacc.Bacc("TRN2", target_bir_lowering=False, num_devices=1)
    arrays = {}

    def give(name, a):
        a = np.ascontiguousarray(a)
        arrays[name] = a
        return nc.dram_tensor(name, a.shape, mybir.dt.from_np(a.dtype), kind="ExternalInput").ap()

    row = np.arange(M * M // 2)
    m, h = row % M, (row % M + row // M + 1) % M
    part_field = np.arange(P)[:, None] % M
    spread = [(part_field == m[i:i + P]) + 1 * (part_field == h[i:i + P]) for i in range(0, len(row), P)]
    spread += [part_field == np.arange(P) % M, np.eye(P)]
    spread = np.stack(spread).astype(ml_dtypes.bfloat16)
    w0 = np.asarray(inputs["L0_rec_W0"])

    args = [
        give("ids", np.asarray(inputs["ids"])),
        [give(f"tbl_{f}", np.asarray(inputs[f"tbl_{f}"])) for f in range(M)],
        give("spread", spread),
        give("w0", w0),
        give("w0_t", w0.transpose(1, 0, 2)),
        give("w0_diag", w0[np.arange(M), np.arange(M)]),
        give("w0_mh", w0[m, h]),
        give("w0_hm", w0[h, m]),
        give("w1", np.asarray(inputs["L0_rec_W1"]).reshape(M * K, K)),
        give("w2", np.asarray(inputs["L0_rec_W2"]).reshape(M * K, K)),
        give("w_top1", np.asarray(inputs["W_top1"])),
        give("b_top1", np.asarray(inputs["b_top1"]).reshape(-1, P).T),
        give("w_top2", np.asarray(inputs["W_top2"])),
        give("b_top2", np.asarray(inputs["b_top2"]).reshape(-1, P).T),
        give("w_top3", np.asarray(inputs["W_top3"]).reshape(-1, P).T),
        give("dense_t", np.asarray(inputs["dense_ctx"]).T),
        nc.dram_tensor("y", (B, 1), mybir.dt.float32, kind="ExternalOutput").ap(),
    ]
    cin_tower(nc, *args)
    got = run_bass_kernel_spmd(nc, [arrays], core_ids=[0])
    return got.results[0]["y"]
```

```python
from contextlib import ExitStack

import concourse.bass as bass
from concourse import mybir

B, M, D, K = 512, 32, 16, 64
P = 128
NCH = B // P
GRP = 512
PAIR = 2 * GRP
COLS = P * D
NT0 = M // 2 // 4 + 1
NQ = NT0 - 1
NT = M * K // P
TG = 2
NG = NT // TG
AHEAD = 2
H1, H2 = 512, 256

RING_V = 5
RING_G = 2
RING_A = 2


class Plan:

    def __init__(self, phases, pool_tiles, gathers, l0_pair1, split, turn, spread, l0_pair0, sums):
        self.phases, self.pool_tiles = phases, pool_tiles
        self.gathers = gathers
        self.l0_pair1 = l0_pair1
        self.split, self.turn, self.spread = split, turn, spread
        self.l0_pair0 = l0_pair0
        self.sums = sums
        self.vector, self.pool = {}, {}
        v = g = 0
        for ph in phases:
            for t in range(NT):
                self.vector[ph, t], self.pool[ph, t] = v, g
                if self.by_pool(ph, t):
                    g += 1
                else:
                    v += 1
        self.vector_total, self.pool_total = v, g

    def by_pool(self, ph, t):
        return t in self.pool_tiles[ph]

    def vector_after(self, ph, t):
        return self.vector[ph, t] + (not self.by_pool(ph, t))

    def pool_after(self, ph, t):
        return self.pool[ph, t] + self.by_pool(ph, t)


SHARED = [(0, 0), (1, 0), (1, 1)]
WARM = 28
STEPS = (0, 11, M // 2)
GATHERS_BEFORE = (8, 7)
BODY = Plan(phases=[(1, 0), (1, 1), (2, 0), (2, 1)],
            pool_tiles={(1, 0): (10, 13), (1, 1): (4, 7, 10, 11), (2, 0): (0, 2, 6, 9, 11, 13), (2, 1): (7, 13)},
            gathers={(1, 0): (11, 5), (1, 1): (1, 0, 0, 0), (2, 0): (0, 0, 0, 0, 0, 0)},
            l0_pair1=[((1, 0), 1), ((1, 0), 2), ((1, 0), 2), ((1, 0), 7), ((1, 0), 8), ((1, 0), 8)],
            split=[((1, 1), 13), ((1, 1), 15)], turn=((2, 0), 0), spread=[((2, 0), 9), ((2, 0), 11)],
            l0_pair0=[((2, 1), 2), ((2, 1), 4), ((2, 1), 4), ((2, 1), 6), ((2, 1), 7), ((2, 1), 9)],
            sums={((1, 0), 6): (0, 0), ((1, 1), 1): (0, 1), ((1, 1), 10): (1, 0), ((2, 0), 8): (1, 1), ((2, 1), 7): (2, 0)})
FIRST = Plan(phases=[(1, 0), (2, 0), (1, 1), (2, 1)],
             pool_tiles={(1, 0): (11,), (2, 0): (6, 9, 12, 14), (1, 1): (1, 2, 5, 7, 10, 12, 13), (2, 1): (7, 13)},
             gathers={(1, 0): (0,), (2, 0): (10, 5, 2, 0), (1, 1): (0, 0, 0, 0, 0, 0, 0)},
             l0_pair1=[((1, 0), 8), ((1, 0), 9), ((1, 0), 10), ((1, 0), 10), ((2, 0), 0), ((2, 0), 0)],
             split=[((1, 1), 0), ((1, 1), 1)], turn=((1, 1), 2), spread=[((1, 1), 7), ((1, 1), 9)],
             l0_pair0=[((1, 1), 12), ((1, 1), 14), ((2, 1), 0), ((2, 1), 0), ((2, 1), 4), ((2, 1), 4)],
             sums={((1, 0), 8): (0, 0), ((2, 0), 9): (0, 1), ((2, 0), 4): (1, 0), ((2, 1), 11): (1, 1), ((1, 1), 4): (2, 0)})
PAIR1_SPLIT, PAIR1_TURN, PAIR1_SPREAD = [((1, 0), 2), ((1, 0), 3), ((1, 0), 4)], ((1, 0), 5), ((1, 0), 7)
LAST = Plan(phases=[(1, 0), (1, 1), (2, 0), (2, 1)],
            pool_tiles={(1, 0): (4, 7, 12), (1, 1): (2, 5, 8, 11), (2, 0): (2, 3, 8, 11, 12), (2, 1): (3, 6, 10, 13, 14)},
            gathers=None,
            l0_pair1=[((1, 0), 1), ((1, 0), 3), ((1, 0), 4), ((1, 0), 5), ((1, 0), 9), ((1, 0), 10)],
            split=[], turn=None, spread=[], l0_pair0=[],
            sums={((1, 0), 6): (0, 0), ((1, 1), 3): (0, 1), ((1, 1), 8): (1, 0), ((2, 0), 15): (1, 1), ((2, 1), 11): (2, 0)})
SUM_BEFORE = ((1, 0), 4)

VN, GN = BODY.vector_total, BODY.pool_total
AN = 2 * NT0
assert VN % RING_V == 0 and GN % RING_G == 0 and AN % RING_A == 0
assert (FIRST.vector_total, FIRST.pool_total) == (VN, GN)
assert FIRST.phases[3] == BODY.phases[3] and FIRST.pool_tiles[2, 1] == BODY.pool_tiles[2, 1]
assert sum(sum(g) for g in FIRST.gathers.values()) == sum(sum(g) for g in BODY.gathers.values()) \
    == M - sum(GATHERS_BEFORE)


def cin_tower(nc, ids, table, base, base_first, spread, w0, w0_t, w0_diag, w0_mh, w0_hm, w1, w2, w_top1, b_top1,
              w_top2, b_top2, w_top3, dense_t, out):
    f32, bf16, i32 = mybir.dt.float32, mybir.dt.bfloat16, mybir.dt.int32
    ALU, ACT, AX = mybir.AluOpType, mybir.ActivationFunctionType, mybir.AxisListType
    ctx = ExitStack()
    with ctx:
        def sb(name, shape, dt=f32):
            return ctx.enter_context(nc.sbuf_tensor(name, shape, dt))

        def ps(name, shape, dt=f32):
            return ctx.enter_context(nc.psum_tensor(name, shape, dt))

        def sem(name):
            return ctx.enter_context(nc.semaphore(name))

        x0_dram = nc.dram_tensor("x0_dram", (NCH, 2, M, PAIR), f32, kind="Internal").ap()

        x0b = sb("x0b", [P, 2, NT, PAIR])
        w1_sb = sb("w1_sb", [P, NT, K])
        w2_sb = sb("w2_sb", [P, NT, K])
        w0_sb = sb("w0_sb", [P, NT0, K])
        spread_sb = sb("spread_sb", [P, NT0 + 1, P], bf16)
        ids_all = sb("ids_all", [P, NCH, M], i32)
        ids_first = sb("ids_first", [P, 2, M // 2], i32)
        ids_sb = sb("ids_sb", [P, M], i32)
        rows = sb("rows", [P, M, D])
        parts = sb("parts", [P, D, 4, M], bf16)
        parts_t = sb("parts_t", [P, COLS], bf16)
        x0_rows = sb("x0_rows", [2 * M, PAIR])
        x_pool = sb("x_pool", [P, 2, PAIR])
        z_v = sb("z_v", [P, RING_V, PAIR])
        z_g = sb("z_g", [P, RING_G, PAIR])
        z_a = sb("z_a", [P, RING_A, PAIR])
        x3 = sb("x3", [P, PAIR])
        features = sb("features", [P, 2, B])
        wt1_b = sb("wt1_b", [P, H1])
        b1_sb = sb("b1_sb", [P, H1 // P])
        b2_sb = sb("b2_sb", [P, H2 // P])
        raw = z_g[:, 0, 0:M * D].rearrange("p (q j d) -> p q j d", q=2, d=D)
        rows_first = z_a[:, 0, 0:M * D].rearrange("p (h j d) -> p h j d", h=2, d=D)
        base_sb = z_g[:, 1, 0:M].bitcast(i32)
        base_first_sb = z_g[:, 1, M:M + M // 2].bitcast(i32)
        early = x0b[:, 1, :, :].rearrange("p t c -> p (t c)")
        w0_all = early[0:M, 0:M * K]
        w0_all_t = early[0:M, M * K:2 * M * K]
        w0_sum = early[0:M, 2 * M * K:2 * M * K + K]
        w0_twice = early[0:M, 2 * M * K + K:2 * M * K + 2 * K]
        w0_add = early[:, 2 * M * K + 2 * K:2 * M * K + 2 * K + (NT0 - 1) * K].rearrange("p (t k) -> p t k", k=K)
        late = x0b[:, 0, :, :].rearrange("p t c -> p (t c)")
        wt1_a = late[:, 0:H1]
        wt2 = late[:, 3072:4096].rearrange("p (t n) -> p t n", n=H2)
        wt3 = late[:, 4096:4098]
        h1 = late[:, 5120:5120 + H1 // P * B].rearrange("p (t c) -> p t c", c=B)
        h2 = late[:, 7168:7168 + H2 // P * B].rearrange("p (t c) -> p t c", c=B)
        y_sb = late[:, 8192:8192 + P]

        acc = ps("acc", [P, 2, GRP])
        x_ps = ps("x_ps", [P, 2, PAIR])
        q_ps = ps("q_ps", [P, PAIR])
        turned = q_ps[:, :].bitcast(bf16)

        ids_in, ids_all_in, ids_ready = sem("ids_in"), sem("ids_all_in"), sem("ids_ready")
        consts_in, w0_in, w1_in, w2_in, top_in = (sem(n) for n in ("consts_in", "w0_in", "w1_in", "w2_in", "top_in"))
        zero_done, w0_step, w0_ready = sem("zero_done"), sem("w0_step"), sem("w0_ready")
        gathered = sem("gathered")
        part0_done, rest1_done, part1_done = sem("part0_done"), sem("rest1_done"), sem("part1_done")
        split_done = sem("split_done")
        turn_done, parts_t_done = sem("turn_done"), sem("parts_t_done")
        spread_done, x0_rows_done = sem("spread_done"), sem("x0_rows_done")
        x0_stored = [sem(f"x0_stored_{p}") for p in range(2)]
        x0b_in = [[sem(f"x0b_in_{p}_{g}") for g in range(NG)] for p in range(2)]
        q_ready = sem("q_ready")
        z_v_made, z_g_made, z_a_made = sem("z_v_made"), sem("z_g_made"), sem("z_a_made")
        z_v_free, z_g_free, z_a_free = sem("z_v_free"), sem("z_g_free"), sem("z_a_free")
        x_ps_done = [sem(f"x_ps_done_{p}") for p in range(2)]
        acts_out = [sem(f"acts_out_{p}") for p in range(2)]
        acts_free = [sem(f"acts_free_{p}") for p in range(2)]
        gathered_first = [sem(f"gathered_first_{i}") for i in range(3)]
        ids_first_ready, ids_all_ready = sem("ids_first_ready"), sem("ids_all_ready")
        top_b_in = sem("top_b_in")
        shifted_a, shifted_v = sem("shifted_a"), sem("shifted_v")
        split_first = [sem(f"split_first_{p}") for p in range(2)]
        turn_first = [sem(f"turn_first_{p}") for p in range(2)]
        parts_t_a = [sem(f"parts_t_a_{p}") for p in range(2)]
        parts_t_first = sem("parts_t_first")
        x_ps_half = sem("x_ps_half")
        mlp_mm, mlp_act, y_done, y_out = sem("mlp_mm"), sem("mlp_act"), sem("y_done"), sem("y_out")
        sp_step, pool_step = sem("sp_step"), sem("pool_step")

        def q_buffer(pair, j):
            return q_ps[:, :] if j % 2 == 1 else x_ps[:, pair, :]

        first_q = [x_ps[:, 0, :], q_ps[:, :], x_ps[:, 1, :], x_ps[:, 0, :]]

        def first_part(k, p, h, js):
            return parts[p * K:(p + 1) * K, :, k, h * M // 2 + js.start:h * M // 2 + js.stop]\
                .rearrange("p d j -> p j d")

        def layer0_z(n, first):
            return z_v[:, n % NQ, :] if first else z_a[:, n % RING_A, :]

        def all_gathered(c):
            return 16 * M * c

        def steps_at(hooks, ph, t):
            for at, step in hooks:
                if at == (ph, t):
                    step()

        block = ctx.enter_context(nc.Block())

        @block.sync
        def _(sp):
            def store(c, p):
                sp.wait_ge(x0_rows_done, 2 * c + p + 1)
                sp.sem_inc(sp_step, 1)
                sp.dma_start(x0_dram[c, p], x0_rows[M * p:M * p + M, :]).then_inc(x0_stored[p], 16)

            def load(c, p, g):
                for t in range(TG * g, TG * (g + 1)):
                    src = x0_dram[c, p, 2 * t:2 * t + 2, :]
                    src = src.rearrange("m (o n) -> m o n", o=1).to_broadcast([2, K, PAIR])
                    sp.dma_start(x0b[:, p, t, :], src).then_inc(x0b_in[p][g], 16)

            def x0_round_trip(c):
                for p in range(2):
                    store(c, p)
                for p in range(2):
                    sp.wait_ge(x0_stored[p], 16 * (c + 1))
                    sp.sem_inc(sp_step, 1)
                    for g in range(NG):
                        at = (2, p), TG * g + TG - 1
                        sp.wait_ge(z_v_made, (c - 1) * VN + max(FIRST.vector_after(*at), BODY.vector_after(*at)))
                        sp.sem_inc(sp_step, 1)
                        sp.wait_ge(z_g_made, (c - 1) * GN + max(FIRST.pool_after(*at), BODY.pool_after(*at)))
                        sp.sem_inc(sp_step, 1)
                        load(c, p, g)

            for h in range(2):
                sp.dma_start(ids_first[h * K:(h + 1) * K, :, :],
                             ids[0:P, h * M // 2:(h + 1) * M // 2].rearrange("(q b) j -> b q j", q=2))\
                    .then_inc(ids_in, 16)
            sp.dma_start(base_first_sb, base_first).then_inc(ids_in, 16)
            sp.dma_start(ids_all[:, :, :], ids.rearrange("(c p) f -> p c f", p=P)).then_inc(ids_all_in, 16)
            sp.dma_start(base_sb, base).then_inc(ids_all_in, 16)

            store(0, 0)
            sp.wait_ge(x0_stored[0], 16)
            for i in range(2 * NG):
                p, g = divmod(i, NG)
                if i == NG - 2:
                    store(0, 1)
                if i == NG:
                    sp.wait_ge(x0_stored[1], 16)
                    sp.wait_ge(w0_ready, 1)
                if i >= AHEAD:
                    sp.wait_ge(x0b_in[(i - AHEAD) // NG][(i - AHEAD) % NG], 16 * TG)
                load(0, p, g)
            with sp.Fori(0, NCH - 1) as c:
                x0_round_trip(c + 1)

            sp.wait_ge(z_v_made, (NCH - 1) * VN + LAST.vector_after((2, 0), NT - 1))
            sp.wait_ge(z_g_made, (NCH - 1) * GN + LAST.pool_after((2, 0), NT - 1))
            sp.dma_start(wt1_a, w_top1[0:P, :]).then_inc(top_in, 16)
            sp.dma_start(wt2, w_top2.rearrange("(t p) n -> p t n", p=P)).then_inc(top_in, 16)
            sp.dma_start(wt3, w_top3).then_inc(top_in, 16)
            sp.wait_ge(y_done, 1)
            sp.dma_start(out.rearrange("(c b) o -> c (o b)", b=P), y_sb[0:P:P // NCH, :]).then_inc(y_out, 16)
            sp.wait_ge(y_out, 16)

        @block.gpsimd
        def _(pool):
            def start_gathers(c):
                if isinstance(c, int):
                    pool.wait_ge(ids_all_ready, 1)
                else:
                    pool.wait_ge(gathered, all_gathered(c - 1))
                pool.tensor_copy(ids_sb[:, :], ids_all[:, bass.ds(c, 1), :].rearrange("p c f -> p (c f)"))\
                    .then_inc(ids_ready, 1)
                pool.wait_ge(ids_ready, c)
                pool.sem_inc(pool_step, 1)
                if not isinstance(c, int):
                    pool.wait_ge(split_done, c - 1)
                    pool.sem_inc(pool_step, 1)

            def gather(f):
                pool.indirect_dma_start(rows[:, f, :], None, table,
                                        bass.IndirectOffsetOnAxis(ids_sb[:, f:f + 1], 0)).then_inc(gathered, 16)

            def phase(ph, c, count, field, gathers=None):
                layer, p = ph
                for n, t in enumerate(count.pool_tiles[ph]):
                    for _ in range(gathers[n] if gathers else 0):
                        gather(field)
                        field += 1
                    if n == 0:
                        pool.wait_ge(acts_out[p], 3 * c + layer + p)
                    pool.wait_ge(x0b_in[p][t // TG], 16 * TG * (c + 1))
                    k = count.pool[ph, t]
                    pool.wait_ge(z_g_free, c * GN + k + 1)
                    pool.tensor_tensor(z_g[:, k % RING_G, :], x_pool[:, p, :], x0b[:, p, t, :],
                                       ALU.mult).then_inc(z_g_made, 1)
                return field

            def from_layer1(c, count, field):
                for ph in count.phases[:3]:
                    field = phase(ph, c, count, field, count.gathers and count.gathers[ph])

            pool.wait_ge(ids_first_ready, 1)
            for p in range(2):
                for j in range(M // 2):
                    pool.indirect_dma_start(raw[:, p, j, :], None, table,
                                            bass.IndirectOffsetOnAxis(ids_first[:, p, j:j + 1], 0))\
                        .then_inc(gathered_first[2 if p else int(j >= STEPS[1])], 16)
            start_gathers(1)
            for f in range(sum(GATHERS_BEFORE)):
                gather(f)
            pool.wait_ge(split_first[1], 1)
            from_layer1(0, FIRST, sum(GATHERS_BEFORE))
            with pool.Fori(1, NCH - 1) as c:
                start_gathers(c + 1)
                field = phase((2, 1), c - 1, BODY, 0, GATHERS_BEFORE)
                from_layer1(c, BODY, field)
            phase((2, 1), NCH - 2, BODY, 0)
            from_layer1(NCH - 1, LAST, 0)
            phase((2, 1), NCH - 1, LAST, 0)

        @block.scalar
        def _(act):
            act.dma_start(spread_sb[:, :, :], spread.rearrange("t k p -> k t p")).then_inc(consts_in, 16)
            act.dma_start(w0_sb[:, 0:NT0 - 1, :], w0_mh.rearrange("(t p) k -> p t k", p=P)).then_inc(w0_in, 16)
            act.dma_start(w0_add, w0_hm.rearrange("(t p) k -> p t k", p=P)).then_inc(w0_in, 16)
            act.dma_start(w0_all, w0.rearrange("m h k -> m (h k)")).then_inc(w0_in, 16)
            act.dma_start(w0_all_t, w0_t.rearrange("m h k -> m (h k)")).then_inc(w0_in, 16)
            act.dma_start(w0_twice, w0_diag).then_inc(w0_in, 16)
            act.dma_start(w1_sb[:, :, :], w1.rearrange("(t p) k -> p t k", p=P)).then_inc(w1_in, 16)
            act.dma_start(w2_sb[:, :, :], w2.rearrange("(t p) k -> p t k", p=P)).then_inc(w2_in, 16)
            act.wait_ge(zero_done, 4)
            act.dma_start(wt1_b[0:K + D, :], w_top1[P:3 * K + D, :]).then_inc(top_b_in, 16)
            act.dma_start(features[K:K + D, 1, :], dense_t).then_inc(top_b_in, 16)
            act.dma_start(b1_sb[:, :], b_top1).then_inc(consts_in, 16)
            act.dma_start(b2_sb[:, :], b_top2).then_inc(consts_in, 16)

            def part0(lo=0, hi=M):
                act.activation(parts[:, :, 0, lo:hi].rearrange("p d m -> p m d"), rows[:, lo:hi, :],
                               ACT.Copy).then_inc(part0_done, 1)

            def part1(lo=0, hi=M):
                act.activation(parts[:, :, 1, lo:hi].rearrange("p d m -> p m d"), rows[:, lo:hi, :],
                               ACT.Copy).then_inc(part1_done, 1)

            def turn(c):
                act.wait_ge(turn_done, c)
                for p in range(2):
                    act.activation(parts_t[:, p * PAIR:(p + 1) * PAIR].rearrange("p (d b) -> p d b", b=K),
                                   turned.rearrange("p (d q b) -> p q d b", q=2, b=K)[:, p, :, :],
                                   ACT.Copy).then_inc(parts_t_done, 1)

            def save_x0(c, p):
                act.wait_ge(spread_done, 2 * c + p + 1)
                act.activation(x0_rows[M * p:M * p + M, :], q_ps[0:M, :], ACT.Copy).then_inc(x0_rows_done, 1)

            def squares(c, p, tiles=range(NT0)):
                first = isinstance(c, int) and (c, p) == (0, 0)
                for t in tiles:
                    n = p * NT0 + t
                    if not first:
                        act.wait_ge(z_a_free, c * AN + n + 1)
                    elif t == NQ:
                        act.wait_ge(z_a_free, RING_A + 1)
                    if t < NQ:
                        act.wait_ge(q_ready, (c * 2 + p) * NQ + t + 1)
                        act.activation(layer0_z(n, first), first_q[t] if first else q_buffer(p, t),
                                       ACT.Square).then_inc(z_a_made, 1)
                    else:
                        act.wait_ge(x0_rows_done, 2 * c + p + 1)
                        act.activation(layer0_z(n, first)[0:M, :], x0_rows[M * p:M * p + M, :],
                                       ACT.Square).then_inc(z_a_made, 1)

            def evict(layer, p, c, count=None):
                if layer == 0:
                    act.wait_ge(z_a_free, RING_A + c * AN + (p + 1) * NT0)
                else:
                    act.wait_ge(z_v_free, RING_V + c * VN + count.vector_after((layer, p), NT - 1))

                def relu(dst, half, groups=(0, 1)):
                    for grp in groups:
                        last = act.activation(dst[half * K:(half + 1) * K, grp * GRP:(grp + 1) * GRP],
                                              acc[grp * K:(grp + 1) * K, p, :], ACT.Relu)
                    return last

                if isinstance(c, int) and c == 0 and (layer, p) in SHARED:
                    relu(x_ps[:, p, :], 0, [0])
                    relu(x_ps[:, p, :], 1, [0]).then_inc(x_ps_done[p], 1)
                    act.wait_ge(x_ps_half, SHARED.index((layer, p)) + 1)
                elif layer < 2:
                    relu(x_ps[:, p, :], 0)
                    relu(x_ps[:, p, :], 1).then_inc(x_ps_done[p], 1)
                act.wait_ge(acts_free[p], 3 * c + layer + 1)
                if layer < 2:
                    relu(x_pool[:, p, :], 0)
                    relu(x_pool[:, p, :], 1).then_inc(acts_out[p], 1)
                else:
                    relu(x3, p).then_inc(acts_out[p], 1)

            act.sem_inc(acts_out[1], 1)
            def first_parts(step, p, lo, hi):
                mine, js = slice(p * K, (p + 1) * K), slice(lo, hi)
                act.wait_ge(gathered_first[step], 16 * (hi - lo))
                act.activation(rows_first[mine, 0, js, :], raw[0:K, p, js, :], ACT.Copy).then_inc(shifted_a, 1)
                act.wait_ge(shifted_a, step + 1)
                act.wait_ge(shifted_v, step + 1)
                for k, made in ((0, part0_done), (1, part1_done)):
                    if k == 1:
                        act.wait_ge(rest1_done, step + 1)
                    for h in range(2):
                        last = act.activation(first_part(k, p, h, js), rows_first[mine, h, js, :], ACT.Copy)
                    last.then_inc(made, 1)

            for i in range(2):
                first_parts(i, 0, *STEPS[i:i + 2])
            act.wait_ge(turn_first[0], 1)
            act.activation(parts_t[:, 0:GRP], turned[:, 0:GRP], ACT.Copy).then_inc(parts_t_a[0], 1)
            squares(0, 0)
            evict(0, 0, 0)
            first_parts(2, 1, 0, M // 2)
            act.wait_ge(turn_first[1], 1)
            act.activation(parts_t[:, PAIR:COLS], turned[:, 0:PAIR], ACT.Copy).then_inc(parts_t_a[1], 1)
            save_x0(0, 1)

            def next_split(c):
                act.wait_ge(gathered, all_gathered(c + 1))
                part0()
                act.wait_ge(rest1_done, c + 4)
                part1()

            def next_x0(c):
                turn(c + 1)
                save_x0(c + 1, 0)
                save_x0(c + 1, 1)

            def chunk(c, count, last):
                squares(c, 1)
                evict(0, 1, c)
                evict(1, 0, c, count)
                if not last:
                    next_split(c)
                evict(1, 1, c, count)
                if not last:
                    next_x0(c)
                evict(2, 0, c, count)
                if not last:
                    squares(c + 1, 0)
                    evict(0, 0, c + 1)
                evict(2, 1, c, count)

            squares(0, 1)
            evict(1, 0, 0, FIRST)
            evict(0, 1, 0)
            next_split(0)
            evict(2, 0, 0, FIRST)
            act.wait_ge(x0_stored[1], 16)
            next_x0(0)
            squares(1, 0, range(3))
            evict(1, 1, 0, FIRST)
            squares(1, 0, range(3, NT0))
            evict(0, 0, 1)
            evict(2, 1, 0, FIRST)

            with act.Fori(1, NCH - 1) as c:
                chunk(c, BODY, False)
            chunk(NCH - 1, LAST, True)

            act.wait_ge(consts_in, 48)
            for n in range(H1 // P):
                act.wait_ge(mlp_mm, n + 1)
                act.activation(h1[:, n, :], x_ps[:, n // 2, (n % 2) * GRP:(n % 2 + 1) * GRP], ACT.Relu,
                               bias=b1_sb[:, n:n + 1]).then_inc(mlp_act, 1)
            for n in range(H2 // P):
                act.wait_ge(mlp_mm, H1 // P + n + 1)
                act.activation(h2[:, n, :], q_ps[:, n * GRP:(n + 1) * GRP], ACT.Relu,
                               bias=b2_sb[:, n:n + 1]).then_inc(mlp_act, 1)
            act.wait_ge(mlp_mm, (H1 + H2) // P + 1)
            act.activation(y_sb, acc[:, 0, 0:P], ACT.Copy).then_inc(y_done, 1)

        @block.vector
        def _(dve):
            dve.wait_ge(ids_in, 48)
            dve.tensor_tensor(ids_first[:, :, :], ids_first[:, :, :],
                              base_first_sb.rearrange("p (o j) -> p o j", o=1).to_broadcast([P, 2, M // 2]),
                              ALU.add).then_inc(ids_first_ready, 1)
            dve.memset(parts[:, :, 3, :], 0.0).then_inc(zero_done, 1)
            dve.memset(w0_sb[:, NQ, :], 0.0).then_inc(zero_done, 1)
            dve.memset(wt1_b[K:P, :], 0.0).then_inc(zero_done, 1)
            dve.memset(features[K:P, 1, :], 0.0).then_inc(zero_done, 1)
            dve.wait_ge(ids_all_in, 32)
            dve.tensor_tensor(ids_all[:, :, :], ids_all[:, :, :],
                              base_sb.rearrange("p (o f) -> p o f", o=1).to_broadcast([P, NCH, M]),
                              ALU.add).then_inc(ids_all_ready, 1)
            for p in range(2):
                dve.sem_inc(acts_free[p], 1)
            dve.wait_ge(w0_in, 80)
            w0_pairs = w0_sb[:, 0:NT0 - 1, :]
            dve.tensor_tensor(w0_pairs, w0_pairs, w0_add, ALU.add).then_inc(w0_step, 1)
            dve.tensor_tensor(w0_all, w0_all, w0_all_t, ALU.add).then_inc(w0_step, 1)
            dve.wait_ge(w0_step, 2)
            dve.tensor_scalar(w0_pairs, w0_pairs, 0.5, None, ALU.mult).then_inc(w0_step, 1)
            dve.tensor_reduce(w0_sum, w0_all.rearrange("m (h k) -> m k h", k=K), AX.X, ALU.add).then_inc(w0_step, 1)
            dve.tensor_scalar(w0_twice, w0_twice, 2.0, None, ALU.mult).then_inc(w0_step, 1)
            dve.wait_ge(w0_step, 5)
            twice = w0_sb[P - M:P, NT0 - 2, :]
            dve.tensor_scalar(twice, twice, 0.5, None, ALU.mult).then_inc(w0_step, 1)
            dve.wait_ge(zero_done, 2)
            dve.scalar_tensor_tensor(w0_sb[0:M, NT0 - 1, :], w0_sum, -0.5, w0_twice, ALU.mult,
                                     ALU.add).then_inc(w0_step, 1)
            dve.wait_ge(w0_step, 7)
            dve.sem_inc(w0_ready, 1)

            def split1(n, lo=0, hi=M):
                dve.wait_ge(part0_done, n)
                dve.tensor_tensor(rows[:, lo:hi, :], rows[:, lo:hi, :],
                                  parts[:, :, 0, lo:hi].rearrange("p d m -> p m d"),
                                  ALU.subtract).then_inc(rest1_done, 1)

            def split2(n, lo=0, hi=M):
                dve.wait_ge(part1_done, n)
                return dve.tensor_tensor(parts[:, :, 2, lo:hi].rearrange("p d m -> p m d"), rows[:, lo:hi, :],
                                         parts[:, :, 1, lo:hi].rearrange("p d m -> p m d"), ALU.subtract)

            def sums(layer, p, c):
                n = 3 * c + layer
                dve.wait_ge(acts_out[p], n + 1 + p)
                half = slice(K, P) if layer == 1 else slice(0, K)
                src = x3[p * K:(p + 1) * K, :] if layer == 2 else x_pool[half, p, :]
                src = src.rearrange("p (d b) -> p b d", b=K)
                dst = features[half, layer // 2, bass.ds(c * P + p * K, K)]
                dve.tensor_reduce(dst, src, AX.X, ALU.add).then_inc(acts_free[p], 1)

            def first_rests(step, p, lo, hi):
                mine, js = slice(p * K, (p + 1) * K), slice(lo, hi)

                def shift():
                    dve.wait_ge(gathered_first[step], 16 * (hi - lo))
                    dve.tensor_copy(rows_first[mine, 1, js, :], raw[K:P, p, js, :]).then_inc(shifted_v, 1)

                def rest1():
                    dve.wait_ge(part0_done, step + 1)
                    for h in range(2):
                        last = dve.tensor_tensor(rows_first[mine, h, js, :], rows_first[mine, h, js, :],
                                                 first_part(0, p, h, js), ALU.subtract)
                    last.then_inc(rest1_done, 1)

                def rest2():
                    dve.wait_ge(part1_done, step + 1)
                    for h in range(2):
                        last = dve.tensor_tensor(first_part(2, p, h, js), rows_first[mine, h, js, :],
                                                 first_part(1, p, h, js), ALU.subtract)
                    if hi == M // 2:
                        last.then_inc(split_first[p], 1)

                return [shift, rest1, rest2]

            def half_x(layer, p):
                for half in range(2):
                    made = dve.tensor_scalar(x_ps[half * K:(half + 1) * K, p, GRP:PAIR], acc[K:P, p, :], 0.0,
                                             None, ALU.max)
                made.then_inc(x_ps_half, 1)
                dve.wait_ge(x_ps_half, SHARED.index((layer, p)) + 1)

            def chunk(c, count, first, last):
                hooks = [(at, lambda lp=lp: sums(*lp, c)) for at, lp in count.sums.items()]
                if first:
                    hooks += zip(PAIR1_SPLIT, first_rests(2, 1, 0, M // 2))
                else:
                    hooks.append((SUM_BEFORE, lambda: sums(2, 1, c - 1)))
                if not last:
                    hooks += [(count.split[0], lambda: split1(c + 4)),
                              (count.split[1], lambda: split2(c + 4).then_inc(split_done, 1))]
                for ph in count.phases:
                    layer, p = ph
                    for t in range(NT):
                        steps_at(hooks, ph, t)
                        if count.by_pool(ph, t):
                            continue
                        k = count.vector[ph, t]
                        if t == 0 and first and (layer - 1, p) in SHARED[1:]:
                            dve.wait_ge(z_v_free, RING_V + count.vector_after((layer - 1, p), NT - 1))
                            half_x(layer - 1, p)
                        if t == 0:
                            dve.wait_ge(x_ps_done[p], 2 * c + layer)
                        if count.vector[ph, TG * (t // TG)] == k:
                            dve.wait_ge(x0b_in[p][t // TG], 16 * TG * (c + 1))
                        dve.wait_ge(z_v_free, c * VN + k + 1)
                        dve.tensor_tensor(z_v[:, k % RING_V, :], x_ps[:, p, :], x0b[:, p, t, :],
                                          ALU.mult).then_inc(z_v_made, 1)

            for i in range(2):
                for step in first_rests(i, 0, *STEPS[i:i + 2]):
                    step()
            dve.wait_ge(turn_first[0], 2)
            dve.tensor_copy(parts_t[:, GRP:PAIR], turned[:, PAIR:PAIR + GRP]).then_inc(parts_t_first, 1)
            dve.wait_ge(spread_done, 1)
            dve.tensor_copy(x0_rows[0:M, :], acc[0:M, :, :].rearrange("p n c -> p (n c)")).then_inc(x0_rows_done, 1)
            dve.wait_ge(z_a_free, RING_A + NT0)
            half_x(0, 0)
            chunk(0, FIRST, True, False)
            with dve.Fori(1, NCH - 1) as c:
                chunk(c, BODY, False, False)
            chunk(NCH - 1, LAST, False, True)
            sums(2, 1, NCH - 1)

        @block.tensor
        def _(pe):
            pe.wait_ge(consts_in, 48)
            pe.wait_ge(zero_done, 2)
            ident = spread_sb[:, NT0, :]
            pe.sem_inc(z_v_free, RING_V)
            pe.sem_inc(z_g_free, RING_G)
            pe.sem_inc(z_a_free, RING_A)

            def turn_parts(c):
                pe.wait_ge(split_done, c)
                for d in range(D):
                    last = pe.transpose(turned[:, d * P:(d + 1) * P],
                                        parts[:, d, :, :].rearrange("p k m -> p (k m)"), ident)
                last.then_inc(turn_done, 1)

            def turn_first_pair(p):
                mine = slice(p * K, (p + 1) * K)
                pe.wait_ge(split_first[p], 1)
                for d in range(D):
                    col = d * K + (PAIR - GRP) * (p == 0 and d >= D // 2)
                    last = pe.transpose(turned[:, col:col + K], parts[mine, d, :, :].rearrange("p k m -> p (k m)"),
                                        ident[mine, mine])
                    if d == D - 1 or p == 0 and d == D // 2 - 1:
                        last.then_inc(turn_first[p], 1)

            def spread_to(dst, j, p):
                for n in range(2):
                    cols = slice(p * PAIR + n * GRP, p * PAIR + (n + 1) * GRP)
                    last = pe.matmul(dst[:, n * GRP:(n + 1) * GRP], spread_sb[:, j, :], parts_t[:, cols],
                                     start=True, stop=True)
                return last

            def spread_x0(c, p):
                if p == 0:
                    pe.wait_ge(parts_t_done, 2 * c)
                else:
                    pe.wait_ge(x0_rows_done, 2 * c + 1)
                spread_to(q_ps[:, :], NQ, p).then_inc(spread_done, 1)

            def spread_first_pair1():
                pe.wait_ge(parts_t_a[1], 1)
                spread_to(q_ps[:, :], NQ, 1).then_inc(spread_done, 1)

            def multiply(w, z, p, start, stop):
                for grp in range(2):
                    last = pe.matmul(acc[grp * K:(grp + 1) * K, p, :], w, z[:, grp * GRP:(grp + 1) * GRP],
                                     start=start, stop=stop)
                return last

            def layer0_steps(c, p):
                def first():
                    if p == 0:
                        pe.wait_ge(x0_rows_done, 2 * (c + 1))
                    else:
                        pe.wait_ge(z_a_made, c * AN + NT0)
                        if isinstance(c, int) and c == 0:
                            pe.wait_ge(x0_rows_done, 2)
                    for j in range(2):
                        spread_to(q_buffer(p, j), j, p).then_inc(q_ready, 1)
                    pe.wait_ge(acts_out[p], 3 * c + 1 if p else 3 * c)

                def tile(t):
                    n = p * NT0 + t
                    pe.wait_ge(z_a_made, c * AN + n + 1)
                    if t + 2 < NQ:
                        spread_to(q_buffer(p, t + 2), t + 2, p).then_inc(q_ready, 1)
                    multiply(w0_sb[:, t, :], layer0_z(n, False), p, t == 0, t == NT0 - 1).then_inc(z_a_free, 1)

                return [first] + [lambda t=t: tile(t) for t in range(NT0)]

            def chunk(c, count, last):
                hooks = list(zip(count.l0_pair1, layer0_steps(c, 1)))
                if count is FIRST:
                    hooks += [(PAIR1_TURN, lambda: turn_first_pair(1)), (PAIR1_SPREAD, spread_first_pair1)]
                if not last:
                    hooks += [(count.turn, lambda: turn_parts(c + 1)), (count.spread[0], lambda: spread_x0(c + 1, 0)),
                              (count.spread[1], lambda: spread_x0(c + 1, 1))]
                    hooks += zip(count.l0_pair0, layer0_steps(c + 1, 0))
                for ph in count.phases:
                    layer, p = ph
                    w = (w1_sb, w2_sb)[layer - 1]
                    for t in range(NT):
                        steps_at(hooks, ph, t)
                        if t == 0:
                            pe.wait_ge(acts_out[p], 3 * c + layer + p)
                        if count.by_pool(ph, t):
                            k = count.pool[ph, t]
                            pe.wait_ge(z_g_made, c * GN + k + 1)
                            z, used = z_g[:, k % RING_G, :], z_g_free
                        else:
                            k = count.vector[ph, t]
                            pe.wait_ge(z_v_made, c * VN + k + 1)
                            z, used = z_v[:, k % RING_V, :], z_v_free
                        multiply(w[:, t, :], z, p, t == 0, t == NT - 1).then_inc(used, 1)

            pe.wait_ge(gathered_first[0], 16 * STEPS[1])
            for _ in range(WARM):
                pe.matmul(acc[:, 0, 0:P], ident, ident, start=True, stop=True)
            turn_first_pair(0)
            pe.wait_ge(parts_t_a[0], 1)
            pe.wait_ge(parts_t_first, 1)
            spread_to(first_q[0], 0, 0).then_inc(q_ready, 1)
            spread_to(acc[:, :, :].rearrange("p n c -> p (n c)"), NQ, 0).then_inc(spread_done, 1)
            for j in (1, 2):
                spread_to(first_q[j], j, 0).then_inc(q_ready, 1)
            pe.wait_ge(w0_ready, 1)
            pe.wait_ge(x0_rows_done, 1)
            for t in range(NT0):
                pe.wait_ge(z_a_made, t + 1)
                multiply(w0_sb[:, t, :], layer0_z(t, True), 0, t == 0, t == NT0 - 1).then_inc(z_a_free, 1)
                if t == 0:
                    spread_to(first_q[3], 3, 0).then_inc(q_ready, 1)
            pe.wait_ge(w1_in, 16)
            pe.wait_ge(w2_in, 16)
            chunk(0, FIRST, False)
            with pe.Fori(1, NCH - 1) as c:
                chunk(c, BODY, False)
            chunk(NCH - 1, LAST, True)

            def hidden1(n):
                return x_ps[:, n // 2, (n % 2) * GRP:(n % 2 + 1) * GRP]

            pe.wait_ge(top_in, 48)
            pe.wait_ge(top_b_in, 32)
            for p in range(2):
                pe.wait_ge(acts_free[p], 3 * NCH)
            for n in range(H1 // P):
                pe.matmul(hidden1(n), wt1_a[:, n * P:(n + 1) * P], features[:, 0, :], start=True, stop=False)
            for cols in (slice(0, B - P), slice(B - P, B)):
                if cols.stop == B:
                    for p in range(2):
                        pe.wait_ge(acts_free[p], 3 * NCH + 1)
                for n in range(H1 // P):
                    last = pe.matmul(hidden1(n)[:, cols], wt1_b[:, n * P:(n + 1) * P], features[:, 1, cols],
                                     start=False, stop=cols.stop == B)
                    if cols.stop == B:
                        last.then_inc(mlp_mm, 1)
            for t in range(H1 // P):
                pe.wait_ge(mlp_act, t + 1)
                for n in range(H2 // P):
                    last = pe.matmul(q_ps[:, n * GRP:(n + 1) * GRP], wt2[:, t, n * P:(n + 1) * P], h1[:, t, :],
                                     start=(t == 0), stop=(t == H1 // P - 1))
                    if t == H1 // P - 1:
                        last.then_inc(mlp_mm, 1)
            pe.wait_ge(acts_out[0], 3 * NCH)
            for t in range(H2 // P):
                pe.wait_ge(mlp_act, H1 // P + t + 1)
                for c in range(NCH):
                    last = pe.matmul(acc[c * P // NCH:c * P // NCH + 1, 0, 0:P], wt3[:, t:t + 1],
                                     h2[:, t, c * P:(c + 1) * P], start=(t == 0), stop=(t == H2 // P - 1))
            last.then_inc(mlp_mm, 1)


def kernel(**inputs):
    import ml_dtypes
    import numpy as np
    import concourse.bacc as bacc
    from concourse.bass_utils import run_bass_kernel_spmd

    nc = bacc.Bacc("TRN2", target_bir_lowering=False, num_devices=1)
    arrays = {}

    def give(name, a):
        a = np.ascontiguousarray(a)
        arrays[name] = a
        return nc.dram_tensor(name, a.shape, mybir.dt.from_np(a.dtype), kind="ExternalInput").ap()

    row = np.arange(M * M // 2)
    m, h = row % M, (row % M + row // M + 1) % M
    part_field = np.arange(P)[:, None] % M
    spread = [(part_field == m[i:i + P]) + 1 * (part_field == h[i:i + P]) for i in range(0, len(row), P)]
    spread += [part_field == np.arange(P) % M, np.eye(P)]
    spread = np.stack(spread).astype(ml_dtypes.bfloat16)
    w0 = np.asarray(inputs["L0_rec_W0"])

    tables = [np.asarray(inputs[f"tbl_{f}"]) for f in range(M)]
    base = np.cumsum([0] + [len(t) for t in tables[:-1]]).astype(np.int32)

    args = [
        give("ids", np.asarray(inputs["ids"])),
        give("table", np.concatenate(tables)),
        give("base", np.tile(base, (P, 1))),
        give("base_first", base.reshape(2, M // 2).repeat(K, axis=0)),
        give("spread", spread),
        give("w0", w0),
        give("w0_t", w0.transpose(1, 0, 2)),
        give("w0_diag", w0[np.arange(M), np.arange(M)]),
        give("w0_mh", w0[m, h]),
        give("w0_hm", w0[h, m]),
        give("w1", np.asarray(inputs["L0_rec_W1"]).reshape(M * K, K)),
        give("w2", np.asarray(inputs["L0_rec_W2"]).reshape(M * K, K)),
        give("w_top1", np.asarray(inputs["W_top1"])),
        give("b_top1", np.asarray(inputs["b_top1"]).reshape(-1, P).T),
        give("w_top2", np.asarray(inputs["W_top2"])),
        give("b_top2", np.asarray(inputs["b_top2"]).reshape(-1, P).T),
        give("w_top3", np.asarray(inputs["W_top3"]).reshape(-1, P).T),
        give("dense_t", np.asarray(inputs["dense_ctx"]).T),
        nc.dram_tensor("y", (B, 1), mybir.dt.float32, kind="ExternalOutput").ap(),
    ]
    cin_tower(nc, *args)
    got = run_bass_kernel_spmd(nc, [arrays], core_ids=[0])
    return got.results[0]["y"]
```
